# Optimizing a Trainium2 kernel written in Bass

```python
import numpy as np
import jax
import jax.numpy as jnp

def _softmax(x, axis=-1):
    return jax.nn.softmax(x, axis=axis)

def _gelu(x):
    return jax.nn.gelu(x, approximate=True)

def _silu(x):
    return jax.nn.silu(x)

def _sigmoid(x):
    return jax.nn.sigmoid(x)

def _layernorm(x, axis=-1, eps=1e-05):
    m = jnp.mean(x, axis=axis, keepdims=True)
    v = jnp.var(x, axis=axis, keepdims=True)
    return (x - m) / jnp.sqrt(v + eps)

def _scatter_add(tgt, idx, src, axis=0):
    return tgt.at[idx].add(src)

def _segment_sum(src, seg, n):
    return jax.ops.segment_sum(src, seg, n)
kernel_name = 'mk_hybrid_d1_jaxref_r8_f1d7cb'

def setup_inputs(seed: int=0):
    np.random.seed(seed)
    _w = jnp.asarray

    def _L0_attn_a_setup():
        import jax, jax.numpy as jnp
        import numpy as np
        HIDDEN = 256
        NUM_HEADS = 6
        HEAD_V = 64
        VALUE_DIM = NUM_HEADS * HEAD_V
        CONV_K = 4
        PHASE_BASE = 10000.0
        EPS = 1e-05

        def _causal_depthwise_conv(x, w):
            B, T, C = x.shape
            K = w.shape[1]
            xp = jnp.pad(x, ((0, 0), (K - 1, 0), (0, 0)))
            y = jnp.zeros_like(x)
            for j in range(K):
                y = y + xp[:, j:j + T, :] * w[:, j]
            return y

        def _rotate(x, ang):
            cos = jnp.cos(ang)
            sin = jnp.sin(ang)
            xe = x[..., ::2]
            xo = x[..., 1::2]
            ye = xe * cos - xo * sin
            yo = xo * cos + xe * sin
            return jnp.stack([ye, yo], axis=-1).reshape(x.shape)

        def _forward(hidden_states, Wq, Wk, Wv, Wa, Wb, Wg, Wo, conv_q, conv_k, conv_v, rms_w):
            B, T, _ = hidden_states.shape
            H, D = (NUM_HEADS, HEAD_V)
            inv_freq = 1.0 / PHASE_BASE ** (jnp.arange(0, D, 2, dtype=jnp.float32) / D)
            q = _causal_depthwise_conv(hidden_states @ Wq, conv_q).reshape(B, T, H, D)
            k = _causal_depthwise_conv(hidden_states @ Wk, conv_k).reshape(B, T, H, D)
            v = _causal_depthwise_conv(hidden_states @ Wv, conv_v).reshape(B, T, H, D)
            theta = q[..., ::2] * inv_freq
            psi = k[..., ::2] * inv_freq
            phi = theta - jnp.concatenate([jnp.zeros_like(theta[:, :1]), theta[:, :-1]], axis=1)
            alpha = jax.nn.sigmoid(hidden_states @ Wa)
            beta = jax.nn.sigmoid(hidden_states @ Wb)
            tm = lambda a: jnp.moveaxis(a, 1, 0)
            xs = (tm(theta), tm(psi), tm(phi), tm(v), tm(alpha), tm(beta))

            def step(state, inp):
                th, ps, ph, vt, at, bt = inp
                retained = _rotate(state, ph) * at[..., None]
                write = _rotate(vt, ps)
                new_state = retained + bt[..., None] * write
                out_t = _rotate(new_state, -th)
                return (new_state, out_t)
            state0 = jnp.zeros((B, H, D), hidden_states.dtype)
            _, out = jax.lax.scan(step, state0, xs)
            out = jnp.moveaxis(out, 0, 1)
            g = (hidden_states @ Wg).reshape(B, T, H, D)
            rms = jax.lax.rsqrt(jnp.mean(jnp.square(out), axis=-1, keepdims=True) + EPS)
            o = out * rms * rms_w * jax.nn.silu(g)
            return o.reshape(B, T, VALUE_DIM) @ Wo
        key = jax.random.key(seed)
        ks = jax.random.split(key, 12)
        s = 0.02
        return {'hidden_states': jax.random.normal(ks[0], (2, 256, HIDDEN), jnp.float32), 'Wq': jax.random.normal(ks[1], (HIDDEN, VALUE_DIM), jnp.float32) * s, 'Wk': jax.random.normal(ks[2], (HIDDEN, VALUE_DIM), jnp.float32) * s, 'Wv': jax.random.normal(ks[3], (HIDDEN, VALUE_DIM), jnp.float32) * s, 'Wa': jax.random.normal(ks[4], (HIDDEN, NUM_HEADS), jnp.float32) * s, 'Wb': jax.random.normal(ks[5], (HIDDEN, NUM_HEADS), jnp.float32) * s, 'Wg': jax.random.normal(ks[6], (HIDDEN, VALUE_DIM), jnp.float32) * s, 'Wo': jax.random.normal(ks[7], (VALUE_DIM, HIDDEN), jnp.float32) * s, 'conv_q': jax.random.normal(ks[8], (VALUE_DIM, CONV_K), jnp.float32) * s, 'conv_k': jax.random.normal(ks[9], (VALUE_DIM, CONV_K), jnp.float32) * s, 'conv_v': jax.random.normal(ks[10], (VALUE_DIM, CONV_K), jnp.float32) * s, 'rms_w': jnp.ones((HEAD_V,), jnp.float32)}
    _L0_attn_a_in = _L0_attn_a_setup()

    def _L0_attn_b_setup():
        import jax, jax.numpy as jnp
        import numpy as np
        NUM_HEADS = 16
        WINDOW = 128
        PERSIST = 16
        key = jax.random.key(seed)
        ks = jax.random.split(key, 6)
        B, S, D, L = (2, 256, 256, 64)
        sd = 1.0 / np.sqrt(D)
        sl = 1.0 / np.sqrt(L)
        return {'x': jax.random.normal(ks[0], (B, S, D), dtype=jnp.float32), 'Wq': jax.random.normal(ks[1], (D, D), dtype=jnp.float32) * sd, 'Wkv': jax.random.normal(ks[2], (D, L), dtype=jnp.float32) * sd, 'Wk': jax.random.normal(ks[3], (L, D), dtype=jnp.float32) * sl, 'Wv': jax.random.normal(ks[4], (L, D), dtype=jnp.float32) * sl, 'Wo': jax.random.normal(ks[5], (D, D), dtype=jnp.float32) * sd}
    _L0_attn_b_in = _L0_attn_b_setup()

    def _L0_ffn_setup():
        import jax, jax.numpy as jnp
        import numpy as np
        from jax import lax
        TOP_K = 2
        NORM_TOPK = True
        W_SCALE = 0.02
        key = jax.random.key(seed)
        k1, k2, k3, k4 = jax.random.split(key, 4)
        B, S, D = (4, 256, 256)
        E, H = (8, 176)
        x = jax.random.normal(k1, (B, S, D), dtype=jnp.float32)
        gate_up_proj = jax.random.normal(k2, (E, 2 * H, D), dtype=jnp.float32) * W_SCALE
        down_proj = jax.random.normal(k3, (E, D, H), dtype=jnp.float32) * W_SCALE
        router_w = jax.random.normal(k4, (E, D), dtype=jnp.float32) * W_SCALE
        return {'x': x, 'gate_up_proj': gate_up_proj, 'down_proj': down_proj, 'router_w': router_w}
    _L0_ffn_in = _L0_ffn_setup()
    _d = {'L0_attn_a_hidden_states': _L0_attn_a_in['hidden_states'], 'L0_attn_a_Wq': _L0_attn_a_in['Wq'], 'L0_attn_a_Wk': _L0_attn_a_in['Wk'], 'L0_attn_a_Wv': _L0_attn_a_in['Wv'], 'L0_attn_a_Wa': _L0_attn_a_in['Wa'], 'L0_attn_a_Wb': _L0_attn_a_in['Wb'], 'L0_attn_a_Wg': _L0_attn_a_in['Wg'], 'L0_attn_a_Wo': _L0_attn_a_in['Wo'], 'L0_attn_a_conv_q': _L0_attn_a_in['conv_q'], 'L0_attn_a_conv_k': _L0_attn_a_in['conv_k'], 'L0_attn_a_conv_v': _L0_attn_a_in['conv_v'], 'L0_attn_a_rms_w': _L0_attn_a_in['rms_w'], 'L0_attn_b_Wq': _L0_attn_b_in['Wq'], 'L0_attn_b_Wkv': _L0_attn_b_in['Wkv'], 'L0_attn_b_Wk': _L0_attn_b_in['Wk'], 'L0_attn_b_Wv': _L0_attn_b_in['Wv'], 'L0_attn_b_Wo': _L0_attn_b_in['Wo'], 'L0_ffn_gate_up_proj': _L0_ffn_in['gate_up_proj'], 'L0_ffn_down_proj': _L0_ffn_in['down_proj'], 'L0_ffn_router_w': _L0_ffn_in['router_w']}
    _x0 = _d['L0_attn_a_hidden_states']
    _d['L0_attn_a_hidden_states'] = jax.random.normal(jax.random.fold_in(jax.random.key(seed), 1), (1, 2048, 256), dtype=_x0.dtype)
    del _x0
    return _d

def reference(L0_attn_a_hidden_states, L0_attn_a_Wq, L0_attn_a_Wk, L0_attn_a_Wv, L0_attn_a_Wa, L0_attn_a_Wb, L0_attn_a_Wg, L0_attn_a_Wo, L0_attn_a_conv_q, L0_attn_a_conv_k, L0_attn_a_conv_v, L0_attn_a_rms_w, L0_attn_b_Wq, L0_attn_b_Wkv, L0_attn_b_Wk, L0_attn_b_Wv, L0_attn_b_Wo, L0_ffn_gate_up_proj, L0_ffn_down_proj, L0_ffn_router_w):

    def _L0_attn_a_ref(hidden_states, Wq, Wk, Wv, Wa, Wb, Wg, Wo, conv_q, conv_k, conv_v, rms_w):
        import jax, jax.numpy as jnp
        import numpy as np
        HIDDEN = 256
        NUM_HEADS = 6
        HEAD_V = 64
        VALUE_DIM = NUM_HEADS * HEAD_V
        CONV_K = 4
        PHASE_BASE = 10000.0
        EPS = 1e-05

        def _causal_depthwise_conv(x, w):
            B, T, C = x.shape
            K = w.shape[1]
            xp = jnp.pad(x, ((0, 0), (K - 1, 0), (0, 0)))
            y = jnp.zeros_like(x)
            for j in range(K):
                y = y + xp[:, j:j + T, :] * w[:, j]
            return y

        def _rotate(x, ang):
            cos = jnp.cos(ang)
            sin = jnp.sin(ang)
            xe = x[..., ::2]
            xo = x[..., 1::2]
            ye = xe * cos - xo * sin
            yo = xo * cos + xe * sin
            return jnp.stack([ye, yo], axis=-1).reshape(x.shape)

        def _forward(hidden_states, Wq, Wk, Wv, Wa, Wb, Wg, Wo, conv_q, conv_k, conv_v, rms_w):
            B, T, _ = hidden_states.shape
            H, D = (NUM_HEADS, HEAD_V)
            inv_freq = 1.0 / PHASE_BASE ** (jnp.arange(0, D, 2, dtype=jnp.float32) / D)
            q = _causal_depthwise_conv(hidden_states @ Wq, conv_q).reshape(B, T, H, D)
            k = _causal_depthwise_conv(hidden_states @ Wk, conv_k).reshape(B, T, H, D)
            v = _causal_depthwise_conv(hidden_states @ Wv, conv_v).reshape(B, T, H, D)
            theta = q[..., ::2] * inv_freq
            psi = k[..., ::2] * inv_freq
            phi = theta - jnp.concatenate([jnp.zeros_like(theta[:, :1]), theta[:, :-1]], axis=1)
            alpha = jax.nn.sigmoid(hidden_states @ Wa)
            beta = jax.nn.sigmoid(hidden_states @ Wb)
            tm = lambda a: jnp.moveaxis(a, 1, 0)
            xs = (tm(theta), tm(psi), tm(phi), tm(v), tm(alpha), tm(beta))

            def step(state, inp):
                th, ps, ph, vt, at, bt = inp
                retained = _rotate(state, ph) * at[..., None]
                write = _rotate(vt, ps)
                new_state = retained + bt[..., None] * write
                out_t = _rotate(new_state, -th)
                return (new_state, out_t)
            state0 = jnp.zeros((B, H, D), hidden_states.dtype)
            _, out = jax.lax.scan(step, state0, xs)
            out = jnp.moveaxis(out, 0, 1)
            g = (hidden_states @ Wg).reshape(B, T, H, D)
            rms = jax.lax.rsqrt(jnp.mean(jnp.square(out), axis=-1, keepdims=True) + EPS)
            o = out * rms * rms_w * jax.nn.silu(g)
            return o.reshape(B, T, VALUE_DIM) @ Wo
        return _forward(hidden_states, Wq, Wk, Wv, Wa, Wb, Wg, Wo, conv_q, conv_k, conv_v, rms_w)

    def _L0_attn_b_ref(x, Wq, Wkv, Wk, Wv, Wo):
        import jax, jax.numpy as jnp
        import numpy as np
        NUM_HEADS = 16
        WINDOW = 128
        PERSIST = 16
        B, S, D = x.shape
        H = NUM_HEADS
        hd = D // H
        scale = hd ** (-0.5)
        q = (x @ Wq).reshape(B, S, H, hd)
        kv_latent = x @ Wkv
        k = (kv_latent @ Wk).reshape(B, S, H, hd)
        v = (kv_latent @ Wv).reshape(B, S, H, hd)
        qi = jnp.arange(S)[:, None]
        ki = jnp.arange(S)[None, :]
        mask = (ki <= qi) & ((qi - ki < WINDOW) | (ki < PERSIST))
        scores = jnp.einsum('bqhd,bkhd->bhqk', q, k) * scale
        scores = jnp.where(mask[None, None], scores, jnp.finfo(scores.dtype).min)
        attn = jax.nn.softmax(scores, axis=-1)
        out = jnp.einsum('bhqk,bkhd->bqhd', attn, v).reshape(B, S, D)
        return out @ Wo

    def _L0_ffn_ref(x, gate_up_proj, down_proj, router_w):
        import jax, jax.numpy as jnp
        import numpy as np
        from jax import lax
        TOP_K = 2
        NORM_TOPK = True
        W_SCALE = 0.02
        B, S, D = x.shape
        E = gate_up_proj.shape[0]
        h = x.reshape(-1, D)
        T = h.shape[0]
        logits = h @ router_w.T
        probs = jax.nn.softmax(logits.astype(jnp.float32), axis=-1)
        vals, idx = lax.top_k(probs, TOP_K)
        if NORM_TOPK:
            vals = vals / vals.sum(axis=-1, keepdims=True)
        combine = jnp.zeros((T, E), dtype=probs.dtype)
        combine = combine.at[jnp.arange(T)[:, None], idx].add(vals)

        def step(acc, per_expert):
            gup, dp, cw = per_expert
            gate, up = jnp.split(h @ gup.T, 2, axis=-1)
            y = jax.nn.silu(gate) * up @ dp.T
            return (acc + cw[:, None].astype(acc.dtype) * y, None)
        out, _ = lax.scan(step, jnp.zeros_like(h), (gate_up_proj, down_proj, combine.T))
        return out.reshape(B, S, D)
    x = L0_attn_a_hidden_states
    x = x + _L0_attn_a_ref(_layernorm(x, axis=-1), L0_attn_a_Wq, L0_attn_a_Wk, L0_attn_a_Wv, L0_attn_a_Wa, L0_attn_a_Wb, L0_attn_a_Wg, L0_attn_a_Wo, L0_attn_a_conv_q, L0_attn_a_conv_k, L0_attn_a_conv_v, L0_attn_a_rms_w)
    x = x + _L0_ffn_ref(_layernorm(x, axis=-1), L0_ffn_gate_up_proj, L0_ffn_down_proj, L0_ffn_router_w)
    x = x + _L0_attn_b_ref(_layernorm(x, axis=-1), L0_attn_b_Wq, L0_attn_b_Wkv, L0_attn_b_Wk, L0_attn_b_Wv, L0_attn_b_Wo)
    x = x + _L0_ffn_ref(_layernorm(x, axis=-1), L0_ffn_gate_up_proj, L0_ffn_down_proj, L0_ffn_router_w)
    return x

_drawn_inputs = setup_inputs


def setup_inputs(seed=0):
    import zlib

    import numpy as np

    out = dict(_drawn_inputs(seed))
    spreads = {'L0_attn_a_rms_w': (1.0, 0.6)}
    factors = {'L0_attn_a_Wq': 8.0,
     'L0_attn_a_Wk': 8.0,
     'L0_attn_a_Wa': 8.0,
     'L0_attn_a_Wb': 7.878,
     'L0_attn_a_conv_q': 8.0,
     'L0_attn_a_conv_k': 8.0,
     'L0_ffn_gate_up_proj': 2.679,
     'L0_ffn_router_w': 2.892}
    for name, (base, spread) in spreads.items():
        noise = np.random.default_rng([zlib.crc32(name.encode()), seed]).standard_normal(out[name].shape)
        drawn = base * np.exp(spread * noise) if base else spread * noise
        out[name] = jnp.asarray(drawn.astype(out[name].dtype))
    for name, factor in factors.items():
        out[name] = (out[name] * factor).astype(out[name].dtype)
    return out
```

```python
from contextlib import ExitStack

import numpy as np

import concourse.bass as bass
from concourse import mybir

P = 128
F32 = mybir.dt.float32
F32R = mybir.dt.float32r
ALU = mybir.AluOpType
ACT = mybir.ActivationFunctionType
AX = mybir.AxisListType

T, D = 2048, 256
KD = D // P
CH = 512
NCH = T // CH
TPC = CH // P
PAD = 4
EPS = 1e-5

HA, HV, TAPS = 6, 64, 4
UNITS = 2
VT, GT = 4, 3

NE, FH = 8, 176
FT = NE * FH // P

HB, HD = 16, 16
LAT = 64
PERSIST = 16
WIN = PERSIST + 2 * P
HG = HB // 2
STK = 3 * HD
MASKED = -1e30

MAGIC = 12582912.0
TWO_PI = 6.283185


def now(it, k=1, n=1):
    return (it + 1) * n + k


def before(it, k=1, n=1):
    return it * n + k


def build(nc, t, out, stop=4):
    ctx = ExitStack()
    with ctx:
        def sb(name, shape, dt=F32):
            return ctx.enter_context(nc.sbuf_tensor(name, shape, dt))

        def sem(name):
            return ctx.enter_context(nc.semaphore(name))

        x = sb("x_tok", [P, T // P * D])
        xTh = sb("xTh", [P, KD, PAD + T], F32R)
        xTl = sb("xTl", [P, KD, PAD + T], F32R)
        xn = sb("xn", [P, TPC, D])
        stats = sb("stats", [P, TPC, 6])
        meanvar = sb("meanvar", [P, TPC, 2])
        rstd = sb("rstd", [P, TPC])
        vareps = sb("vareps", [P, TPC])
        minus_half = sb("minus_half", [P, 32])
        ident = sb("ident_sb", [P, P])

        bank = [ctx.enter_context(nc.psum_tensor(f"bank{i}", [P, 2, CH], F32)) for i in range(4)]
        psY = bank[3]
        yT = psY[:].rearrange("p a b -> p (a b)")

        consts_in = sem("consts_in")
        x_in = sem("x_in")

        def xcols(it, t0=0, n=TPC):
            return x[:, bass.ds(it * (TPC * D) + t0 * D, n * D)]

        class Tail:

            def __init__(self, ph, base=0):
                self.turn0 = 0
                self.base = base
                self.y_ready = sem(f"y_ready{ph}")
                self.x_new = sem(f"x_new{ph}")
                self.stat_ready = sem(f"stat{ph}")
                self.mv_ready = sem(f"mv{ph}")
                self.vareps_ready = sem(f"vareps{ph}")
                self.rstd_ready = sem(f"rstd{ph}")
                self.xn_ready = sem(f"xn{ph}")
                self.xT_ready = sem(f"xT{ph}")
                self.xh_ready = sem(f"xh{ph}")
                self.xl_ready = sem(f"xl{ph}")

        passed = sem("passed")

        def stand(eng):
            eng.sem_inc(passed, 1)

        def credit(eng, *sems):
            for s, n in sems:
                eng.sem_inc(s, n)

        def tail_norm_dve(dve, tl, it, add):
            if add:
                dve.wait_ge(tl.y_ready, now(it + tl.turn0))
                dve.tensor_tensor(xcols(it), yT, xcols(it), ALU.add).then_inc(tl.x_new, 1)
                dve.wait_ge(tl.x_new, now(it + tl.turn0))
            stand(dve)
            for i in range(TPC):
                dve.bn_stats(stats[:, i, :], xcols(it, i, 1)).then_inc(tl.stat_ready, 1)
            dve.wait_ge(tl.stat_ready, now(it + tl.turn0, TPC, TPC))
            stand(dve)
            for i in range(TPC):
                dve.bn_aggr(meanvar[:, i, :], stats[:, i, :]).then_inc(tl.mv_ready, 1)
            dve.wait_ge(tl.mv_ready, now(it + tl.turn0, TPC, TPC))
            dve.wait_ge(tl.rstd_ready, now(it + tl.turn0))
            dve.wait_ge(tl.xT_ready, before(it + tl.turn0))
            for i in range(TPC):
                dve.tensor_scalar(xn[:, i, :], xcols(it, i, 1), meanvar[:, i, 0:1], rstd[:, i:i + 1],
                                  ALU.subtract, ALU.mult).then_inc(tl.xn_ready, 1)

        def tail_split_dve(dve, tl, it):
            dve.wait_ge(tl.xh_ready, now(it + tl.turn0))
            dve.tensor_tensor(xTl[:, :, bass.ds(it * CH + tl.base, CH)], psY[:],
                              xTh[:, :, bass.ds(it * CH + tl.base, CH)].bitcast(F32),
                              ALU.subtract).then_inc(tl.xl_ready, 1)

        def tail_pool(pool, tl, it):
            pool.wait_ge(tl.mv_ready, now(it + tl.turn0, TPC, TPC))
            pool.wait_ge(tl.xn_ready, before(it + tl.turn0, TPC, TPC))
            stand(pool)
            pool.tensor_scalar(vareps[:], meanvar[:, :, 1], EPS, None, ALU.add).then_inc(tl.vareps_ready, 1)
            pool.wait_ge(tl.vareps_ready, now(it + tl.turn0))
            pool.tensor_tensor(rstd[:], vareps[:], minus_half[:, 0:TPC], ALU.pow).then_inc(tl.rstd_ready, 1)

        def tail_pe(pe, tl, it):
            pe.wait_ge(tl.xn_ready, now(it + tl.turn0, TPC, TPC))
            for k in range(KD):
                for i in range(TPC):
                    last = pe.transpose(psY[:, k, i * P:(i + 1) * P], xn[:, i, k * P:(k + 1) * P], ident[:])
            last.then_inc(tl.xT_ready, 1)

        def tail_act(act, tl, it):
            act.wait_ge(tl.xT_ready, now(it + tl.turn0))
            act.activation(xTh[:, :, bass.ds(it * CH + tl.base, CH)], psY[:], ACT.Copy).then_inc(tl.xh_ready, 1)

        t0 = Tail(0, base=PAD)
        zero_pad = sem("zero_pad")
        half_set = sem("half_set")
        padf = sb("padf", [P, KD * PAD])
        with nc.Block() as block:
            @block.sync
            def _(sp):
                sp.dma_start(ident[:], t["ident"]).then_inc(consts_in, 16)
                sp.dma_start(x[:].rearrange("p (t d) -> p t d", d=D),
                             t["x"].rearrange("(t p) d -> p t d", p=P)).then_inc(x_in, 16)

            @block.gpsimd
            def _(pool):
                credit(pool, (t0.rstd_ready, 1), (t0.vareps_ready, 1))
                pool.memset(minus_half[:], -0.5).then_inc(half_set, 1)
                pool.wait_ge(half_set, 1)
                with pool.Fori(0, NCH) as it:
                    tail_pool(pool, t0, it)

            @block.vector
            def _(dve):
                credit(dve, (t0.stat_ready, TPC), (t0.mv_ready, TPC), (t0.xn_ready, TPC), (t0.xl_ready, 1))
                dve.memset(padf[:], 0.0).then_inc(zero_pad, 1)
                dve.wait_ge(zero_pad, 1)
                for w in (xTh, xTl):
                    dve.tensor_copy(w[:, :, 0:PAD], padf[:].rearrange("p (k c) -> p k c", k=KD))\
                       .then_inc(zero_pad, 1)
                dve.wait_ge(x_in, 16)
                with dve.Fori(0, NCH) as it:
                    tail_norm_dve(dve, t0, it, add=False)
                    tail_split_dve(dve, t0, it)

            @block.tensor
            def _(pe):
                credit(pe, (t0.xT_ready, 1))
                pe.wait_ge(consts_in, 16)
                with pe.Fori(0, NCH) as it:
                    pe.wait_ge(t0.xl_ready, before(it))
                    tail_pe(pe, t0, it)

            @block.scalar
            def _(act):
                credit(act, (t0.xh_ready, 1))
                with act.Fori(0, NCH) as it:
                    tail_act(act, t0, it)

        tl = Tail("N")
        if stop > 0:
            recurrence(nc, ctx, t, x, xTh, xTl, yT, psY, bank, tl, stand, credit, tail_norm_dve, tail_split_dve,
                       tail_pool, tail_pe, tail_act, sem, ident, minus_half)
        wts = ffn_weights(nc, ctx, t, sem) if stop > 1 else None
        ffn_sems = {}

        def tail_after(phases):
            tl.turn0 = phases * NCH
            return tl

        if stop > 1:
            experts(nc, t, wts, x, xTh, xTl, yT, psY, bank, tail_after(1), stand, credit, tail_norm_dve, tail_split_dve,
                    tail_pool, tail_pe, tail_act, sem, ident, xcols, ffn_sems, last=False)
        if stop > 2:
            attention(nc, t, x, xTh, xTl, yT, psY, bank, tail_after(2), stand, credit, tail_norm_dve, tail_split_dve,
                      tail_pool, tail_pe, tail_act, sem, ident)
        if stop > 3:
            experts(nc, t, wts, x, xTh, xTl, yT, psY, bank, tail_after(3), stand, credit, tail_norm_dve, tail_split_dve,
                    tail_pool, tail_pe, tail_act, sem, ident, xcols, ffn_sems, last=True)

        stored = sem("stored")
        with nc.Block() as block:
            @block.sync
            def _(sp):
                sp.dma_start(out.rearrange("(t p) d -> p t d", p=P),
                             x[:].rearrange("p (t d) -> p t d", d=D)).then_inc(stored, 16)
                sp.wait_ge(stored, 16)
                if stop == 0:
                    sp.dma_start(t["dbg"].rearrange("(k p) c -> p k c", p=P), xTh[:].bitcast(F32)).then_inc(stored, 16)
                    sp.wait_ge(stored, 32)


def heads_of_tile(u):
    return [p // 32 if u == 0 else 4 + (p % 64) // 32 for p in range(P)]


def recurrence(nc, octx, t, x, xTh, xTl, yT, psY, bank, tl, stand, credit, tail_norm_dve, tail_split_dve,
               tail_pool, tail_pe, tail_act, osem, ident, minus_half):
    ctx = ExitStack()
    with ctx:
        def sb(name, shape, dt=F32):
            return ctx.enter_context(nc.sbuf_tensor(name, shape, dt))

        sem = osem
        wfh, wfl = sb("wfh", [P, KD, TAPS, 2 * P], F32R), sb("wfl", [P, KD, TAPS, 2 * P], F32R)
        wvh, wvl = sb("wvh", [P, KD, VT * P], F32R), sb("wvl", [P, KD, VT * P], F32R)
        wgh, wgl = sb("wgh", [P, KD, GT * P], F32R), sb("wgl", [P, KD, GT * P], F32R)
        woh, wol = sb("woh", [P, GT, D], F32R), sb("wol", [P, GT, D], F32R)
        wabh, wabl = sb("wabh", [P, KD, 2 * HA], F32R), sb("wabl", [P, KD, 2 * HA], F32R)
        sel = sb("sel", [2 * HA, 4, P], F32R)
        selr = sb("selr", [8, 2, P], F32R)
        headsum = sb("headsum", [P, 2, 8])
        convv = sb("convv", [P, VT, TAPS])
        rmsw = sb("rmsw", [P, GT])
        sscale = sb("sscale", [P, 2])

        prep = ExitStack()

        def pb(name, shape, dt=F32):
            return prep.enter_context(nc.sbuf_tensor(name, shape, dt))

        wq_raw, wk_raw = pb("wq_raw", [P, KD, 2 * P]), pb("wk_raw", [P, KD, 2 * P])
        cq_raw, ck_raw = pb("cq_raw", [P, TAPS, 2 * P]), pb("ck_raw", [P, TAPS, 2 * P])
        freq = pb("freq", [P, 2 * P])
        wv_raw, wg_raw = pb("wv_raw", [P, KD, VT * P]), pb("wg_raw", [P, KD, GT * P])
        wo_raw, wab_raw = pb("wo_raw", [P, GT, D]), pb("wab_raw", [P, KD, 2 * HA])
        sel_raw, selr_raw = pb("sel_raw", [2 * HA, 4, P]), pb("selr_raw", [8, 2, P])
        kq, qq = pb("kq", [P, KD, TAPS, 2 * P]), pb("qq", [P, KD, TAPS, 2 * P])

        a_in = sem("a_in")
        prep_dve = sem("prep_dve")
        prep_pool = sem("prep_pool")
        with nc.Block() as block:
            loads = [(wk_raw[:], t["wk"].rearrange("(k p) m -> p k m", p=P)),
                     (ck_raw[:], t["ck"].rearrange("(o j) m -> o j m", o=1).broadcast_to([P, TAPS, 2 * P])),
                     (freq[:], t["freq"].broadcast_to([P, 2 * P])),
                     (wq_raw[:], t["wq"].rearrange("(k p) m -> p k m", p=P)),
                     (cq_raw[:], t["cq"].rearrange("(o j) m -> o j m", o=1).broadcast_to([P, TAPS, 2 * P])),
                     (wv_raw[:], t["wv"].rearrange("(k p) m -> p k m", p=P)),
                     (wg_raw[:], t["wg"].rearrange("(k p) m -> p k m", p=P)),
                     (wo_raw[:], t["wo"].rearrange("(k p) m -> p k m", p=P)),
                     (wab_raw[:], t["wab"].rearrange("(k p) m -> p k m", p=P)),
                     (sel_raw[:], t["sel"]), (selr_raw[:], t["selr"]),
                     (headsum[:], t["headsum"]), (convv[:], t["convv"]), (rmsw[:], t["rmsw"]),
                     (sscale[:], t["sscale"])]

            @block.sync
            def _(sp):
                for dst, src in loads:
                    sp.dma_start(dst, src).then_inc(a_in, 16)

            @block.vector
            def _(dve):
                n = 0

                def link(ins):
                    nonlocal n
                    n += 1
                    ins.then_inc(prep_dve, 1)
                    dve.wait_ge(prep_dve, n)
                dve.wait_ge(a_in, 16 * len(loads))
                link(dve.tensor_tensor(ck_raw[:], ck_raw[:], freq[:].unsqueeze(1).broadcast_to([P, TAPS, 2 * P]), ALU.mult))
                for k in range(KD):
                    link(dve.tensor_tensor(kq[:, k], ck_raw[:], wk_raw[:, k].unsqueeze(1).broadcast_to([P, TAPS, 2 * P]), ALU.mult))
                dve.wait_ge(prep_pool, 1 + KD)
                link(dve.tensor_tensor(kq[:], kq[:], qq[:], ALU.subtract))
                link(dve.tensor_copy(wfh[:], kq[:]))
                link(dve.tensor_tensor(wfl[:], kq[:], wfh[:].bitcast(F32), ALU.subtract))
                link(dve.tensor_copy(sel[:], sel_raw[:]))
                link(dve.tensor_copy(selr[:], selr_raw[:]))
                for h, l, raw in ((wvh, wvl, wv_raw), (wabh, wabl, wab_raw)):
                    link(dve.tensor_copy(h[:], raw[:]))
                    link(dve.tensor_tensor(l[:], raw[:], h[:].bitcast(F32), ALU.subtract))

            @block.gpsimd
            def _(pool):
                n = 0

                def link(ins):
                    nonlocal n
                    n += 1
                    ins.then_inc(prep_pool, 1)
                    pool.wait_ge(prep_pool, n)
                pool.wait_ge(a_in, 16 * len(loads))
                link(pool.tensor_tensor(cq_raw[:], cq_raw[:], freq[:].unsqueeze(1).broadcast_to([P, TAPS, 2 * P]), ALU.mult))
                for k in range(KD):
                    link(pool.tensor_tensor(qq[:, k], cq_raw[:], wq_raw[:, k].unsqueeze(1).broadcast_to([P, TAPS, 2 * P]), ALU.mult))
                for h, l, raw in ((wgh, wgl, wg_raw), (woh, wol, wo_raw)):
                    link(pool.tensor_copy(h[:], raw[:]))
                    link(pool.tensor_tensor(l[:], raw[:], h[:].bitcast(F32), ALU.subtract))
        prep.close()

        whole = sb("whole", [P, 2, CH])
        angle = sb("angle", [P, 2, CH])
        vraw = sb("vraw", [P, VT, PAD + CH])
        vconv = sb("vconv", [P, VT, CH])
        w = sb("w", [P, GT, CH])
        o = sb("o", [P, GT, CH])
        gate = sb("gate", [P, GT, CH])
        sq = sb("sq", [P, GT, CH])
        oh, ol = sb("oh", [P, GT, CH], F32R), sb("ol", [P, GT, CH], F32R)
        carry = sb("carry", [P, GT])
        sg = sb("sg", [2 * HA, CH])
        sgh, sgl = sb("sgh", [2 * HA, CH], F32R), sb("sgl", [2 * HA, CH], F32R)
        ms = sb("ms", [P, TPC * 8])
        rms = sb("rms", [P, TPC * 8])
        rmsh, rmsl = sb("rmsh", [8, CH], F32R), sb("rmsl", [8, CH], F32R)

        psF, psV, psB = bank[0], bank[1], bank[2]
        f_ready = sem("f_ready")
        ab_ready = sem("ab_ready")
        vg_ready = sem("vg_ready")
        beta_ready = sem("beta_ready")
        alpha_ready = sem("alpha_ready")
        ss_ready = sem("ss_ready")
        rT_ready = sem("rT_ready")
        rb_ready = sem("rb_ready")
        sg_ready = sem("sg_ready")
        vg_out = sem("vg_out")
        abs_ready = sem("abs_ready")
        cos_ready = sem("cos_ready")
        sin_ready = sem("sin_ready")
        sq_ready = sem("sq_ready")
        zeroed = sem("zeroed")
        sgh_ready = sem("sgh_ready")
        sgl_ready = sem("sgl_ready")
        whole_ready = sem("whole_ready")
        angle_ready = sem("angle_ready")
        tap_done = sem("tap_done")
        halo_done = sem("halo_done")
        rot_done = sem("rot_done")
        scan_done = sem("scan_done")
        carry_done = sem("carry_done")
        gated = sem("gated")
        ms_ready = sem("ms_ready")
        rms_ready = sem("rms_ready")
        rh_ready = sem("rh_ready")
        rl_ready = sem("rl_ready")
        o2_ready = sem("o2_ready")
        oh_ready = sem("oh_ready")
        ol_ready = sem("ol_ready")
        NVG = VT + GT
        NTAP = VT * TAPS
        NROT = 8

        with nc.Block() as block:
            @block.tensor
            def _(pe):
                credit(pe, (vg_ready, NVG), (f_ready, 1), (ab_ready, 1), (beta_ready, 1), (alpha_ready, 1),
                       (ss_ready, 1), (rT_ready, 1), (rb_ready, 1), (tl.y_ready, 1), (tl.xT_ready, 1))
                with pe.Fori(0, NCH) as it:
                    pe.wait_ge(o2_ready, before(it, GT, GT))
                    for u in range(UNITS):
                        n = 0
                        for j in range(TAPS):
                            for k in range(KD):
                                cols = bass.ds(it * CH + PAD - TAPS + 1 + j, CH)
                                for wt, xx in ((wfh, xTh), (wfl, xTh), (wfh, xTl)):
                                    last = pe.matmul(psF[:, u], wt[:, k, j, u * P:(u + 1) * P], xx[:, k, cols],
                                                     start=n == 0, stop=n == 3 * KD * TAPS - 1)
                                    n += 1
                    last.then_inc(f_ready, 1)

                    def project(dst, wh, wl, c0, c1):
                        n = 0
                        for k in range(KD):
                            cols = bass.ds(it * CH + PAD, CH)
                            for wt, xx in ((wh, xTh), (wl, xTh), (wh, xTl)):
                                last = pe.matmul(dst, wt[:, k, c0:c1], xx[:, k, cols],
                                                 start=n == 0, stop=n == 3 * KD - 1)
                                n += 1
                        return last

                    pe.wait_ge(rl_ready, before(it))
                    stand(pe)
                    project(psB[0:2 * HA, 0], wabh, wabl, 0, 2 * HA).then_inc(ab_ready, 1)
                    for i in range(NVG):
                        pe.wait_ge(vg_out, now(it, i - 1, NVG))
                        if i < VT:
                            mm = project(psV[:, i % 2], wvh, wvl, i * P, (i + 1) * P)
                        else:
                            mm = project(psV[:, i % 2], wgh, wgl, (i - VT) * P, (i - VT + 1) * P)
                        mm.then_inc(vg_ready, 1)
                        if i == VT - 1:
                            pe.wait_ge(sgl_ready, now(it))
                            for u in range(UNITS):
                                pe.matmul(psB[:, u], sel[:, 2 + u], sgh[:], start=True, stop=False)
                                last = pe.matmul(psB[:, u], sel[:, 2 + u], sgl[:], start=False, stop=True)
                            last.then_inc(beta_ready, 1)
                    pe.wait_ge(angle_ready, now(it))
                    for u in range(UNITS):
                        pe.matmul(psF[:, u], sel[:, u], sgh[:], start=True, stop=False)
                        last = pe.matmul(psF[:, u], sel[:, u], sgl[:], start=False, stop=True)
                    last.then_inc(alpha_ready, 1)
                    pe.wait_ge(sq_ready, now(it))
                    for i in range(TPC):
                        for g in range(GT):
                            last = pe.matmul(psB[:, 0, i * 8:i * 8 + 8], sq[:, g, i * P:(i + 1) * P],
                                             headsum[:, g // 2], start=g == 0, stop=g == GT - 1)
                    last.then_inc(ss_ready, 1)
                    pe.wait_ge(rms_ready, now(it))
                    for i in range(TPC):
                        last = pe.transpose(psB[0:8, 1, i * P:(i + 1) * P], rms[:, i * 8:i * 8 + 8], ident[:])
                    last.then_inc(rT_ready, 1)
                    pe.wait_ge(rl_ready, now(it))
                    for u in range(UNITS):
                        pe.matmul(psF[:, u], selr[:, u], rmsh[:], start=True, stop=False)
                        last = pe.matmul(psF[:, u], selr[:, u], rmsl[:], start=False, stop=True)
                    last.then_inc(rb_ready, 1)
                    pe.wait_ge(ol_ready, now(it))
                    pe.wait_ge(tl.xl_ready, before(it + tl.turn0))
                    for i in range(TPC):
                        n = 0
                        for g in range(GT):
                            for oo, ww in ((oh, woh), (ol, woh), (oh, wol)):
                                last = pe.matmul(yT[:, i * D:(i + 1) * D], oo[:, g, i * P:(i + 1) * P], ww[:, g],
                                                 start=n == 0, stop=n == 3 * GT - 1)
                                n += 1
                    last.then_inc(tl.y_ready, 1)
                    tail_pe(pe, tl, it)

            @block.scalar
            def _(act):
                credit(act, (sg_ready, 1), (vg_out, NVG), (abs_ready, 1), (cos_ready, 1), (sin_ready, 1),
                       (sq_ready, 1), (tl.xh_ready, 1))
                with act.Fori(0, NCH) as it:
                    act.wait_ge(ab_ready, now(it))
                    act.wait_ge(sgl_ready, before(it))
                    act.activation(sg[:], psB[0:2 * HA, 0], ACT.Sigmoid).then_inc(sg_ready, 1)
                    act.wait_ge(halo_done, before(it))
                    for i in range(VT):
                        act.wait_ge(vg_ready, now(it, i + 1, NVG))
                        act.activation(vraw[:, i, PAD:PAD + CH], psV[:, i % 2], ACT.Copy).then_inc(vg_out, 1)
                    act.wait_ge(angle_ready, now(it))
                    act.activation(whole[:], angle[:], ACT.Abs).then_inc(abs_ready, 1)
                    act.wait_ge(abs_ready, now(it))
                    act.activation(whole[:], whole[:], ACT.Sin, bias=sscale[:, 1:2], scale=-TWO_PI)\
                       .then_inc(cos_ready, 1)
                    act.activation(angle[:, 0], angle[:, 0], ACT.Sin, scale=TWO_PI)
                    act.activation(angle[:, 1], angle[:, 1], ACT.Sin, scale=sscale[:, 0:1]).then_inc(sin_ready, 1)
                    act.wait_ge(o2_ready, before(it, GT, GT))
                    for i in range(VT, NVG):
                        act.wait_ge(vg_ready, now(it, i + 1, NVG))
                        act.activation(gate[:, i - VT], psV[:, i % 2], ACT.Silu).then_inc(vg_out, 1)
                    act.wait_ge(scan_done, now(it, GT, GT))
                    act.wait_ge(ol_ready, before(it))
                    act.activation(sq[:], o[:], ACT.Square).then_inc(sq_ready, 1)
                    tail_act(act, tl, it)

            @block.gpsimd
            def _(pool):
                credit(pool, (tl.rstd_ready, 1), (tl.vareps_ready, 1), (rms_ready, 1))
                with pool.Fori(0, NCH) as it:
                    pool.wait_ge(ms_ready, now(it))
                    pool.wait_ge(rT_ready, before(it))
                    pool.tensor_tensor(rms[:], ms[:], minus_half[:, 0:TPC * 8], ALU.pow).then_inc(rms_ready, 1)
                    tail_pool(pool, tl, it)

            @block.vector
            def _(dve):
                credit(dve, (sgh_ready, 1), (sgl_ready, 1), (whole_ready, 1), (angle_ready, 1), (tap_done, NTAP),
                       (halo_done, 1), (rot_done, NROT), (scan_done, GT), (carry_done, 1), (gated, 1), (ms_ready, 1),
                       (rh_ready, 1), (rl_ready, 1), (o2_ready, GT), (oh_ready, 1), (ol_ready, 1), (tl.x_new, 1),
                       (tl.stat_ready, TPC), (tl.mv_ready, TPC), (tl.xn_ready, TPC), (tl.xl_ready, 1))
                dve.memset(vraw[:, :, 0:PAD], 0.0).then_inc(zeroed, 1)
                dve.memset(carry[:], 0.0).then_inc(zeroed, 1)
                dve.wait_ge(zeroed, 2)
                with dve.Fori(0, NCH) as it:
                    dve.wait_ge(sg_ready, now(it))
                    dve.wait_ge(alpha_ready, before(it))
                    dve.tensor_copy(sgh[:], sg[:]).then_inc(sgh_ready, 1)
                    dve.wait_ge(sgh_ready, now(it))
                    dve.tensor_tensor(sgl[:], sg[:], sgh[:].bitcast(F32), ALU.subtract).then_inc(sgl_ready, 1)
                    dve.wait_ge(f_ready, now(it))
                    dve.tensor_scalar(whole[:], psF[:], MAGIC, -MAGIC, ALU.add, ALU.add).then_inc(whole_ready, 1)
                    dve.wait_ge(whole_ready, now(it))
                    dve.tensor_tensor(angle[:], psF[:], whole[:], ALU.subtract).then_inc(angle_ready, 1)
                    for j in range(TAPS):
                        for i in range(VT):
                            src = vraw[:, i, PAD - TAPS + 1 + j:PAD - TAPS + 1 + j + CH]
                            if j == 0:
                                dve.wait_ge(vg_out, now(it, i + 1, NVG))
                                dve.tensor_scalar(vconv[:, i], src, convv[:, i, 0:1], None, ALU.mult)\
                                   .then_inc(tap_done, 1)
                            else:
                                dve.wait_ge(tap_done, now(it, (j - 1) * VT + i + 1, NTAP))
                                dve.scalar_tensor_tensor(vconv[:, i], src, convv[:, i, j:j + 1], vconv[:, i],
                                                         ALU.mult, ALU.add).then_inc(tap_done, 1)
                    dve.tensor_copy(vraw[:, :, 1:PAD], vraw[:, :, CH + 1:CH + PAD]).then_inc(halo_done, 1)
                    dve.wait_ge(tap_done, now(it, NTAP, NTAP))
                    dve.wait_ge(sin_ready, now(it))
                    cos01 = whole[:, 0].unsqueeze(1).broadcast_to([P, 2, CH])
                    dve.tensor_tensor(o[:, 0:2], vconv[:, 0:2], cos01, ALU.mult).then_inc(rot_done, 1)
                    dve.tensor_tensor(o[:, 2], vconv[:, 2], whole[:, 1], ALU.mult).then_inc(rot_done, 1)
                    dve.tensor_tensor(w[:, 0], vconv[:, 1], angle[:, 0], ALU.mult).then_inc(rot_done, 1)
                    dve.tensor_tensor(w[:, 1], vconv[:, 0], angle[:, 0], ALU.mult).then_inc(rot_done, 1)
                    dve.tensor_tensor(w[:, 2], vconv[:, 3], angle[:, 1], ALU.mult).then_inc(rot_done, 1)
                    dve.wait_ge(rot_done, now(it, 5, NROT))
                    dve.tensor_tensor(w[:, 0], o[:, 0], w[:, 0], ALU.subtract).then_inc(rot_done, 1)
                    dve.tensor_tensor(w[:, 1:3], o[:, 1:3], w[:, 1:3], ALU.add).then_inc(rot_done, 1)
                    dve.wait_ge(rot_done, now(it, 7, NROT))
                    dve.wait_ge(beta_ready, now(it))
                    beta01 = psB[:, 0].unsqueeze(1).broadcast_to([P, 2, CH])
                    dve.tensor_tensor(w[:, 0:2], w[:, 0:2], beta01, ALU.mult)
                    dve.tensor_tensor(w[:, 2], w[:, 2], psB[:, 1], ALU.mult).then_inc(rot_done, 1)
                    dve.wait_ge(rot_done, now(it, 8, NROT))
                    dve.wait_ge(alpha_ready, now(it))
                    dve.wait_ge(carry_done, before(it))
                    for g in range(GT):
                        dve.tensor_tensor_scan(o[:, g], psF[:, g // 2], w[:, g], carry[:, g:g + 1],
                                               ALU.mult, ALU.add).then_inc(scan_done, 1)
                    dve.wait_ge(scan_done, now(it, GT, GT))
                    dve.tensor_copy(carry[:], o[:, :, CH - 1]).then_inc(carry_done, 1)
                    dve.wait_ge(vg_out, now(it, NVG, NVG))
                    dve.tensor_tensor(gate[:], gate[:], o[:], ALU.mult).then_inc(gated, 1)
                    dve.wait_ge(ss_ready, now(it))
                    dve.wait_ge(rms_ready, before(it))
                    dve.tensor_scalar(ms[:], psB[:, 0, 0:TPC * 8], EPS, None, ALU.add).then_inc(ms_ready, 1)
                    dve.wait_ge(rT_ready, now(it))
                    dve.wait_ge(rb_ready, before(it))
                    dve.tensor_copy(rmsh[:], psB[0:8, 1]).then_inc(rh_ready, 1)
                    dve.wait_ge(rh_ready, now(it))
                    dve.tensor_tensor(rmsl[:], psB[0:8, 1], rmsh[:].bitcast(F32), ALU.subtract)\
                       .then_inc(rl_ready, 1)
                    dve.wait_ge(rb_ready, now(it))
                    dve.wait_ge(gated, now(it))
                    for g in range(GT):
                        dve.scalar_tensor_tensor(sq[:, g], gate[:, g], rmsw[:, g:g + 1], psF[:, g // 2],
                                                 ALU.mult, ALU.mult).then_inc(o2_ready, 1)
                    dve.wait_ge(o2_ready, now(it, GT, GT))
                    dve.wait_ge(tl.y_ready, before(it + tl.turn0))
                    dve.tensor_copy(oh[:], sq[:]).then_inc(oh_ready, 1)
                    dve.wait_ge(oh_ready, now(it))
                    dve.tensor_tensor(ol[:], sq[:], oh[:].bitcast(F32), ALU.subtract).then_inc(ol_ready, 1)
                    tail_norm_dve(dve, tl, it, add=True)
                    tail_split_dve(dve, tl, it)


def ffn_weights(nc, octx, t, sem):
    def sb(name, shape, dt=F32R):
        return octx.enter_context(nc.sbuf_tensor(name, shape, dt))

    gu = 2 * FT * P
    wguh, wgul = sb("wguh", [P, KD, gu]), sb("wgul", [P, KD, gu])
    wrh, wrl = sb("wrh", [P, KD, NE]), sb("wrl", [P, KD, NE])
    selcw = sb("selcw", [NE, FT, P])
    lower = sb("lower", [P, NE * NE], F32)
    f_in, f_dve = sem("f_in"), sem("f_dve")
    with nc.sbuf_tensor("gu_raw", [P, KD, gu], F32) as gu_raw, \
         nc.sbuf_tensor("r_raw", [P, KD, NE], F32) as r_raw, nc.sbuf_tensor("s_raw", [NE, FT, P], F32) as s_raw:
        with nc.Block() as block:
            @block.sync
            def _(sp):
                sp.dma_start(gu_raw[:], t["wgu"].rearrange("(k p) m -> p k m", p=P)).then_inc(f_in, 16)
                sp.dma_start(r_raw[:], t["wr"].rearrange("(k p) m -> p k m", p=P)).then_inc(f_in, 16)
                sp.dma_start(s_raw[:], t["selcw"]).then_inc(f_in, 16)
                sp.dma_start(lower[:], t["lower"].broadcast_to([P, NE * NE])).then_inc(f_in, 16)

            @block.vector
            def _(dve):
                dve.wait_ge(f_in, 64)
                dve.tensor_copy(wguh[:], gu_raw[:]).then_inc(f_dve, 1)
                dve.tensor_copy(selcw[:], s_raw[:])
                dve.tensor_copy(wrh[:], r_raw[:]).then_inc(f_dve, 1)
                dve.wait_ge(f_dve, 2)
                dve.tensor_tensor(wgul[:, 0], gu_raw[:, 0], wguh[:, 0].bitcast(F32), ALU.subtract)
                dve.tensor_tensor(wrl[:], r_raw[:], wrh[:].bitcast(F32), ALU.subtract)

            @block.gpsimd
            def _(pool):
                pool.wait_ge(f_dve, 1)
                pool.tensor_tensor(wgul[:, 1], gu_raw[:, 1], wguh[:, 1].bitcast(F32), ALU.subtract)
    return wguh, wgul, wrh, wrl, selcw, lower


def experts(nc, t, wts, x, xTh, xTl, yT, psY, bank, tl, stand, credit, tail_norm_dve, tail_split_dve,
            tail_pool, tail_pe, tail_act, osem, ident, xcols, ffn_sems, last):
    wguh, wgul, wrh, wrl, selcw, lower = wts
    ph = "2" if last else "1"

    def sem(name):
        if name not in ffn_sems:
            ffn_sems[name] = osem(name)
        return ffn_sems[name]
    ctx = ExitStack()
    with ctx:
        def sb(name, shape, dt=F32):
            return ctx.enter_context(nc.sbuf_tensor(name + ph, shape, dt))

        wd_raw = sb("wd_raw", [P, FT, D])
        wdh, wdl = sb("wdh", [P, FT, D], F32R), sb("wdl", [P, FT, D], F32R)
        lg = sb("lg", [NE, CH])
        L = sb("L", [P, TPC, NE])
        top = sb("top", [P, TPC])
        cmp1, cmp2 = sb("cmp1", [P, TPC, NE * NE]), sb("cmp2", [P, TPC, NE * NE])
        rank = sb("rank", [P, TPC, NE])
        chosen = sb("chosen", [P, TPC, NE])
        ex = sb("ex", [P, TPC, NE])
        den, rden = sb("den", [P, TPC]), sb("rden", [P, TPC])
        cw = sb("cw", [P, TPC, NE])
        cwh, cwl = sb("cwh", [NE, CH], F32R), sb("cwl", [NE, CH], F32R)
        silu = sb("silu", [P, 2, CH])
        act_up = sb("act_up", [P, 2, CH])
        hid = sb("hid", [P, 2, CH])
        hh, hl = sb("hh", [P, 2, CH], F32R), sb("hl", [P, 2, CH], F32R)
        psG, psU, psB = bank[0], bank[1], bank[2]

        lg_ready = sem("lg_ready")
        lgT_ready = sem("lgT_ready")
        cwT_ready = sem("cwT_ready")
        g_ready = sem("g_ready")
        u_ready = sem("u_ready")
        b_ready = sem("b_ready")
        down_done = sem("down_done")
        lg_out = sem("lg_out")
        exp_done = sem("exp_done")
        silu_done = sem("silu_done")
        hh_done = sem("hh_done")
        route = sem("route")
        cwl_done = sem("cwl_done")
        up_done = sem("up_done")
        hid_done = sem("hid_done")
        hl_done = sem("hl_done")
        wd_in = sem("wd_in")
        wd_done = sem("wd_done")
        NR = 13
        turns = NCH if last else 0

        with nc.Block() as block:
            @block.tensor
            def _(pe):
                if not last:
                    credit(pe, (lg_ready, 1), (lgT_ready, 1), (cwT_ready, 1), (g_ready, FT), (u_ready, FT),
                           (b_ready, FT), (down_done, FT))
                def project(it, dst, wh, wl, c0, c1):
                    n = 0
                    for k in range(KD):
                        for wt, xx in ((wh, xTh), (wl, xTh), (wh, xTl)):
                            mm = pe.matmul(dst, wt[:, k, c0:c1], xx[:, k, bass.ds(it * CH, CH)],
                                           start=n == 0, stop=n == 3 * KD - 1)
                            n += 1
                    return mm

                def gate_up(it, i):
                    r = it + turns
                    pe.wait_ge(silu_done, now(r, i - 1, FT))
                    project(it, psG[:, i % 2], wguh, wgul, i * P, (i + 1) * P).then_inc(g_ready, 1)
                    pe.wait_ge(up_done, now(r, i - 1, FT))
                    project(it, psU[:, i % 2], wguh, wgul, (FT + i) * P, (FT + i + 1) * P).then_inc(u_ready, 1)

                def head(it, tail_of=None):
                    r = it + turns
                    pe.wait_ge(hid_done, before(r, FT, FT))
                    stand(pe)
                    project(it, psB[0:NE, 0], wrh, wrl, 0, NE).then_inc(lg_ready, 1)
                    gate_up(it, 0)
                    pe.wait_ge(lg_out, now(r))
                    stand(pe)
                    for j in range(TPC):
                        mm = pe.transpose(psB[:, 1, j * NE:(j + 1) * NE], lg[:, j * P:(j + 1) * P],
                                          ident[0:NE, 0:NE])
                    mm.then_inc(lgT_ready, 1)
                    gate_up(it, 1)
                    if tail_of is not None:
                        tail_pe(pe, tl, tail_of)
                    pe.wait_ge(route, now(r, NR, NR))
                    for j in range(TPC):
                        mm = pe.transpose(psB[0:NE, 1, j * P:(j + 1) * P], cw[:, j], ident[:])
                    mm.then_inc(cwT_ready, 1)

                def down(it, i):
                    r = it + turns
                    pe.wait_ge(hl_done, now(r, i + 1, FT))
                    if i == 0:
                        pe.wait_ge(wd_done, 2 * last + 2)
                        pe.wait_ge(tl.xl_ready, before(it + tl.turn0))
                    for j in range(TPC):
                        for n, (h, w) in enumerate(((hh, wdh), (hl, wdh), (hh, wdl))):
                            mm = pe.matmul(yT[:, j * D:(j + 1) * D], h[:, i % 2, j * P:(j + 1) * P], w[:, i],
                                           start=i == 0 and n == 0 and j % 2 == 0,
                                           stop=i == FT - 1 and n == 2, skip_group_check=True)
                    mm.then_inc(down_done, 1)

                def tiles(it):
                    r = it + turns
                    pe.wait_ge(cwl_done, now(r, 2, 2))
                    for i in range(FT):
                        pe.wait_ge(hid_done, now(r, i - 1, FT))
                        pe.matmul(psB[:, i % 2], selcw[:, i], cwh[:], start=True, stop=False)
                        pe.matmul(psB[:, i % 2], selcw[:, i], cwl[:], start=False, stop=True).then_inc(b_ready, 1)
                        if i >= 1:
                            down(it, i - 1)
                        if i + 2 < FT:
                            gate_up(it, i + 2)
                    down(it, FT - 1)
                    pe.wait_ge(down_done, now(r, FT, FT))
                    pe.sem_inc(tl.y_ready, 1)

                head(0)
                with pe.Fori(0, NCH - 1) as it:
                    tiles(it)
                    head(it + 1, tail_of=None if last else it)
                tiles(NCH - 1)
                if not last:
                    tail_pe(pe, tl, NCH - 1)

            @block.scalar
            def _(act):
                if not last:
                    credit(act, (lg_out, 1), (exp_done, 1), (silu_done, FT), (hh_done, FT))
                def gate(it, i):
                    r = it + turns
                    act.wait_ge(g_ready, now(r, i + 1, FT))
                    act.wait_ge(up_done, now(r, i - 1, FT))
                    act.activation(silu[:, i % 2], psG[:, i % 2], ACT.Silu).then_inc(silu_done, 1)

                def head(it, tail_of=None):
                    r = it + turns
                    act.wait_ge(lg_ready, now(r))
                    act.wait_ge(lgT_ready, before(r))
                    act.activation(lg[:], psB[0:NE, 0], ACT.Copy).then_inc(lg_out, 1)
                    gate(it, 0)
                    gate(it, 1)
                    if tail_of is not None:
                        tail_act(act, tl, tail_of)
                    act.wait_ge(route, now(r, 7, NR))
                    act.activation(ex[:], ex[:], ACT.Exp).then_inc(exp_done, 1)

                def tiles(it):
                    r = it + turns
                    for i in range(FT):
                        act.wait_ge(hid_done, now(r, i + 1, FT))
                        act.wait_ge(down_done, now(r, i - 1, FT))
                        act.activation(hh[:, i % 2], hid[:, i % 2], ACT.Copy).then_inc(hh_done, 1)
                        if i + 2 < FT:
                            gate(it, i + 2)

                head(0)
                with act.Fori(0, NCH - 1) as it:
                    tiles(it)
                    head(it + 1, tail_of=None if last else it)
                tiles(NCH - 1)
                if not last:
                    tail_act(act, tl, NCH - 1)

            @block.sync
            def _(sp):
                sp.dma_start(wd_raw[:], t["wd"].rearrange("(k p) m -> p k m", p=P)).then_inc(wd_in, 16)

            @block.gpsimd
            def _(pool):
                pool.wait_ge(wd_in, 16 * (1 + last))
                pool.tensor_copy(wdh[:], wd_raw[:]).then_inc(wd_done, 1)
                pool.wait_ge(wd_done, 2 * last + 1)
                pool.tensor_tensor(wdl[:], wd_raw[:], wdh[:].bitcast(F32), ALU.subtract).then_inc(wd_done, 1)
                if not last:
                    with pool.Fori(0, NCH) as it:
                        tail_pool(pool, tl, it)

            @block.vector
            def _(dve):
                if not last:
                    credit(dve, (route, NR), (cwl_done, 2), (up_done, FT), (hid_done, FT), (hl_done, FT))
                def up(it, i):
                    r = it + turns
                    dve.wait_ge(u_ready, now(r, i + 1, FT))
                    dve.wait_ge(silu_done, now(r, i + 1, FT))
                    dve.wait_ge(hid_done, now(r, i - 1, FT))
                    dve.tensor_tensor(act_up[:, i % 2], silu[:, i % 2], psU[:, i % 2], ALU.mult)\
                       .then_inc(up_done, 1)

                def routing(it, split_of=None):
                    r = it + turns
                    n = 0

                    def step(ins):
                        nonlocal n
                        n += 1
                        ins.then_inc(route, 1)
                        dve.wait_ge(route, now(r, n, NR))

                    by_e = L[:].unsqueeze(3).broadcast_to([P, TPC, NE, NE])
                    by_j = L[:].unsqueeze(2).broadcast_to([P, TPC, NE, NE])
                    low = lower[:].unsqueeze(1).broadcast_to([P, TPC, NE * NE])
                    c1 = cmp1[:].rearrange("p t (e j) -> p t e j", e=NE)
                    c2 = cmp2[:].rearrange("p t (e j) -> p t e j", e=NE)
                    dve.wait_ge(lgT_ready, now(r))
                    step(dve.tensor_copy(L[:], psB[:, 1, 0:TPC * NE].rearrange("p (t e) -> p t e", e=NE)))
                    step(dve.tensor_tensor(c1, by_j, by_e, ALU.is_ge))
                    step(dve.tensor_tensor(cmp1[:], cmp1[:], low, ALU.mult))
                    step(dve.tensor_tensor(c2, by_j, by_e, ALU.is_gt))
                    step(dve.tensor_tensor(cmp1[:], cmp1[:], cmp2[:], ALU.max))
                    step(dve.tensor_reduce(top[:], L[:], AX.X, ALU.max))
                    step(dve.tensor_tensor(ex[:], L[:], top[:].unsqueeze(2).broadcast_to([P, TPC, NE]), ALU.subtract))
                    step(dve.tensor_reduce(rank[:], c1, AX.X, ALU.add))
                    step(dve.tensor_scalar(chosen[:], rank[:], 1.5, None, ALU.is_lt))
                    dve.wait_ge(exp_done, now(r))
                    step(dve.tensor_tensor(chosen[:], chosen[:], ex[:], ALU.mult))
                    step(dve.tensor_reduce(den[:], chosen[:], AX.X, ALU.add))
                    step(dve.reciprocal(rden[:], den[:]))
                    step(dve.tensor_tensor(cw[:], chosen[:], rden[:].unsqueeze(2).broadcast_to([P, TPC, NE]), ALU.mult))
                    assert n == NR
                    if split_of is not None:
                        tail_split_dve(dve, tl, split_of)
                    up(it, 0)
                    up(it, 1)
                    dve.wait_ge(cwT_ready, now(r))
                    dve.tensor_copy(cwh[:], psB[0:NE, 1]).then_inc(cwl_done, 1)
                    dve.wait_ge(cwl_done, now(r, 1, 2))
                    dve.tensor_tensor(cwl[:], psB[0:NE, 1], cwh[:].bitcast(F32), ALU.subtract).then_inc(cwl_done, 1)

                def tiles(it):
                    r = it + turns
                    for i in range(FT):
                        dve.wait_ge(b_ready, now(r, i + 1, FT))
                        dve.wait_ge(up_done, now(r, i + 1, FT))
                        dve.tensor_tensor(hid[:, i % 2], act_up[:, i % 2], psB[:, i % 2], ALU.mult)\
                           .then_inc(hid_done, 1)
                        dve.wait_ge(hh_done, now(r, i + 1, FT))
                        dve.tensor_tensor(hl[:, i % 2], hid[:, i % 2], hh[:, i % 2].bitcast(F32), ALU.subtract)\
                           .then_inc(hl_done, 1)
                        if i + 2 < FT:
                            up(it, i + 2)

                def tail(it, split):
                    if last:
                        dve.wait_ge(tl.y_ready, now(it + tl.turn0))
                        dve.tensor_tensor(xcols(it), yT, xcols(it), ALU.add).then_inc(tl.xl_ready, 1)
                    else:
                        tail_norm_dve(dve, tl, it, add=True)
                        if split:
                            tail_split_dve(dve, tl, it)

                routing(0)
                with dve.Fori(0, NCH - 1) as it:
                    tiles(it)
                    tail(it, split=False)
                    routing(it + 1, split_of=None if last else it)
                tiles(NCH - 1)
                tail(NCH - 1, split=True)


def host_inputs(a):
    ev = np.arange(HV // 2) * 2
    E0 = np.concatenate([h * HV + ev for h in range(4)])
    E1 = np.concatenate([h * HV + ev for h in (4, 5)])
    cols_f = np.concatenate([E0, E1, E1])
    cols_v = np.concatenate([E0, E0 + 1, E1, E1 + 1, E1 + 1, E1])
    cols_g = cols_v[:GT * P]
    inv_freq = (np.float32(1.0) / np.float32(10000.0) ** (np.arange(0, HV, 2, dtype=np.float32) / np.float32(HV)))
    freq = (inv_freq[(cols_f % HV) // 2].astype(np.float64) / (2 * np.pi)).astype(np.float32)[None, :]
    g = lambda n: np.asarray(a["L0_attn_a_" + n])
    sel = np.zeros((2 * HA, 4, P), np.float32)
    selr = np.zeros((8, 2, P), np.float32)
    headsum = np.zeros((P, 2, 8), np.float32)
    for u in range(UNITS):
        for p, h in enumerate(heads_of_tile(u)):
            sel[h, u, p] = 1.0
            sel[HA + h, 2 + u, p] = 1.0
            selr[h, u, p] = 1.0
            headsum[p, u, h] = 1.0 / HV
    sscale = np.empty((P, 2), np.float32)
    sscale[:64, 0], sscale[64:, 0] = -TWO_PI, TWO_PI
    sscale[:, 1] = np.pi / 2
    return {
        "x": g("hidden_states").reshape(T, D),
        "ident": np.eye(P, dtype=np.float32),
        "wq": g("Wq")[:, cols_f], "wk": g("Wk")[:, cols_f],
        "cq": g("conv_q")[cols_f].T, "ck": g("conv_k")[cols_f].T, "freq": freq,
        "wv": g("Wv")[:, cols_v], "wg": g("Wg")[:, cols_g], "wo": g("Wo")[cols_g],
        "wab": np.concatenate([g("Wa"), g("Wb")], 1),
        "sel": sel, "selr": selr, "headsum": headsum,
        "convv": g("conv_v")[cols_v].reshape(VT, P, TAPS).transpose(1, 0, 2),
        "rmsw": g("rms_w")[cols_g % HV].reshape(GT, P).T,
        "sscale": sscale,
        **expert_inputs(a), **attention_inputs(a),
    }


def expert_inputs(a):
    gup = np.asarray(a["L0_ffn_gate_up_proj"])
    selcw = np.zeros((NE, FT, P), np.float32)
    for c in range(FT * P):
        selcw[c // FH, c // P, c % P] = 1.0
    lower = (np.arange(NE)[None, :] < np.arange(NE)[:, None]).astype(np.float32).reshape(1, -1)
    return {
        "wgu": np.concatenate([gup[:, :FH].reshape(NE * FH, D), gup[:, FH:].reshape(NE * FH, D)], 0).T,
        "wd": np.asarray(a["L0_ffn_down_proj"]).transpose(0, 2, 1).reshape(NE * FH, D),
        "wr": np.asarray(a["L0_ffn_router_w"]).T,
        "selcw": selcw, "lower": lower,
    }


def attention(nc, t, x, xTh, xTl, yT, psY, bank, tl, stand, credit, tail_norm_dve, tail_split_dve,
              tail_pool, tail_pe, tail_act, sem, ident):
    ctx = ExitStack()
    NPAIR = TPC * HB // 2
    PPB = HB // 2
    SLOTS = HB // 2
    ROWS = 64 + STK
    SCALE = HD ** -0.5
    KC = PERSIST + P + CH
    with ctx:
        def sb(name, shape, dt=F32):
            return ctx.enter_context(nc.sbuf_tensor("b_" + name, shape, dt))

        shapes = {"bq": [P, KD, D], "bkv": [P, KD, LAT], "bk": [LAT, D], "bv": [LAT, D], "bo": [P, KD, D]}
        wh = {n: sb(n + "h", shapes[n], F32R) for n in shapes}
        wl = {n: sb(n + "l", shapes[n], F32R) for n in shapes}
        masks = sb("masks", [P, TPC, WIN])
        lath, latl = sb("lath", [LAT, CH], F32R), sb("latl", [LAT, CH], F32R)
        qh, ql = sb("qh", [P, KD, CH], F32R), sb("ql", [P, KD, CH], F32R)
        kh, kl = sb("kh", [P, KD, CH], F32R), sb("kl", [P, KD, CH], F32R)
        QS = sb("QS", [ROWS, SLOTS, CH], F32R)
        KS = sb("KS", [ROWS, SLOTS, KC], F32R)
        V = sb("V", [P, TPC + 1, D])
        vp = sb("vp", [PERSIST, D])
        VP = sb("VP", [P, 2, P])
        sm = sb("sm", [P, 4, WIN])
        mx, nmx = sb("mx", [P, 4]), sb("nmx", [P, 4])
        prob = sb("prob", [P, 8, WIN])
        pp = sb("pp", [P, 2, HB, PERSIST])
        rs = sb("rs", [P, 2, HB])
        rinv = sb("rinv", [P, HB])
        pT = sb("pT", [P, 2, 4 * P])
        ppT = sb("ppT", [P, 2 * P])
        on = sb("on", [P, D])
        oTh, oTl = qh, ql
        prep = ExitStack()
        raw = {"bq": pT[:, 0].rearrange("p (k c) -> p k c", k=KD), "bo": pT[:, 1].rearrange("p (k c) -> p k c", k=KD),
               "bk": on[0:LAT], "bv": ppT[0:LAT],
               "bkv": prep.enter_context(nc.sbuf_tensor("b_raw_bkv", shapes["bkv"], F32))[:]}
        zeros = sm[:].rearrange("p a b -> p (a b)")[:, 0:KC]

        psS = [bank[0][:, 0], bank[0][:, 1], bank[1][:, 0], bank[1][:, 1]]
        psT = bank[2]
        psO, psM = psY[:, 0], psY[:, 1]

        b_in = sem("b_in")
        b_prep = sem("b_prep")
        p_lat, p_latl, p_k, p_kl, p_v = (sem("p_" + n) for n in ("lat", "latl", "k", "kl", "v"))
        p_stk = sem("p_stk")
        with nc.Block() as block:
            stack = ((0, 0), (1, 0), (2, 1))

            @block.sync
            def _(sp):
                for n in raw:
                    sp.dma_start(raw[n], t[n].rearrange("(k p) m -> p k m", p=P) if n in ("bq", "bkv", "bo") else t[n])\
                      .then_inc(b_in, 16)
                sp.dma_start(masks[:], t["masks"]).then_inc(b_in, 16)
                sp.wait_ge(p_kl, 2)
                for g in range(KD):
                    for half in range(2):
                        for blk, part in stack:
                            src = (kh, kl)[part][64 * half:64 * half + 64, g, 0:PERSIST]
                            sp.dma_start(KS[64 * half + HD * blk:64 * half + HD * blk + HD, 4 * g:4 * g + 4, 0:PERSIST].bitcast(F32),
                                         src.bitcast(F32)).then_inc(p_stk, 16)
                sp.wait_ge(p_v, 2)
                for h in range(HB):
                    g, r = h // HG, h % HG
                    sp.dma_start(VP[HD * r:HD * r + PERSIST, g, HD * r:HD * r + HD], vp[:, h * HD:(h + 1) * HD])\
                      .then_inc(p_stk, 16)
                sp.wait_ge(p_stk, 16 * (12 + HB))

            @block.vector
            def _(dve):
                n = 0

                def link(ins):
                    nonlocal n
                    n += 1
                    ins.then_inc(b_prep, 1)
                    dve.wait_ge(b_prep, n)
                link(dve.memset(VP[:], 0.0))
                link(dve.memset(V[:, TPC], 0.0))
                dve.wait_ge(b_in, 16 * (len(raw) + 1))
                link(dve.memset(zeros, 0.0))
                for s in range(SLOTS):
                    link(dve.tensor_copy(KS[:, s], zeros[0:ROWS]))
                for m in raw:
                    link(dve.tensor_copy(wh[m][:], raw[m]))
                    link(dve.tensor_tensor(wl[m][:], raw[m], wh[m][:].bitcast(F32), ALU.subtract))
                dve.wait_ge(p_lat, 1)
                dve.tensor_copy(lath[:, 0:PERSIST], psM[0:LAT, 0:PERSIST]).then_inc(p_latl, 1)
                dve.wait_ge(p_latl, 1)
                dve.tensor_tensor(latl[:, 0:PERSIST], psM[0:LAT, 0:PERSIST], lath[:, 0:PERSIST].bitcast(F32),
                                  ALU.subtract).then_inc(p_latl, 1)
                dve.wait_ge(p_k, 1)
                dve.tensor_copy(kh[:, :, 0:PERSIST], bank[0][:, :, 0:PERSIST]).then_inc(p_kl, 1)
                dve.wait_ge(p_kl, 1)
                dve.tensor_tensor(kl[:, :, 0:PERSIST], bank[0][:, :, 0:PERSIST], kh[:, :, 0:PERSIST].bitcast(F32),
                                  ALU.subtract).then_inc(p_kl, 1)
                dve.tensor_copy(vp[:], bank[1][0:PERSIST, 0, 0:D]).then_inc(p_v, 2)

            @block.tensor
            def _(pe):
                pe.wait_ge(b_prep, 2 + 1 + SLOTS + 2 * len(raw))
                n = 0
                for k in range(KD):
                    for w, xx in ((wh, xTh), (wl, xTh), (wh, xTl)):
                        mm = pe.matmul(psM[0:LAT, 0:PERSIST], w["bkv"][:, k], xx[:, k, 0:PERSIST],
                                       start=n == 0, stop=n == 3 * KD - 1)
                        n += 1
                mm.then_inc(p_lat, 1)
                pe.wait_ge(p_latl, 2)
                for n, (w, z) in enumerate(((wh, lath), (wl, lath), (wh, latl))):
                    mm = pe.matmul(bank[1][0:PERSIST, 0, 0:D], z[:, 0:PERSIST], w["bv"][:], start=n == 0, stop=n == 2)
                for g in range(KD):
                    for n, (w, z) in enumerate(((wh, lath), (wl, lath), (wh, latl))):
                        mm = pe.matmul(bank[0][:, g, 0:PERSIST], w["bk"][:, g * P:(g + 1) * P], z[:, 0:PERSIST],
                                       start=n == 0, stop=n == 2)
                mm.then_inc(p_k, 1)

        prep.close()
        lat_ready = sem("lat_ready")
        q_ready = sem("q_ready")
        k_ready = sem("k_ready")
        v_ready = sem("v_ready")
        s_ready = sem("s_ready")
        t_ready = sem("t_ready")
        pv_done = sem("pv_done")
        pt_ready = sem("pt_ready")
        o_ready = sem("o_ready")
        oT_ready = sem("oT_ready")
        lath_done = sem("lath_done")
        qh_done, kh_done = sem("qh_done"), sem("kh_done")
        v_done = sem("v_done")
        e_done = sem("e_done")
        ta_out = sem("ta_out")
        oh_done = sem("boh_done")
        latl_done = sem("latl_done")
        ql_done, kl_done = sem("ql_done"), sem("kl_done")
        m_done = sem("m_done")
        n_done = sem("n_done")
        tv_out = sem("tv_out")
        pp_out = sem("pp_out")
        ri_done = sem("ri_done")
        on_done = sem("on_done")
        ol_done = sem("bol_done")
        mask_done = sem("mask_done")
        halo_done = sem("bhalo_done")
        vhalo_done = sem("vhalo_done")
        pp_done = sem("pp_done")
        stacked = sem("stacked")
        NS = 16 * 24

        STEPS = NPAIR + 6

        def ends_block(p):
            return 0 <= p < NPAIR and p % PPB == PPB - 1

        with nc.Block() as block:
            @block.tensor
            def _(pe):
                credit(pe, (lat_ready, 1), (q_ready, 1), (k_ready, 1), (v_ready, 1), (s_ready, NPAIR),
                       (t_ready, NPAIR), (pv_done, NPAIR), (pt_ready, TPC), (o_ready, TPC), (oT_ready, TPC))
                with pe.Fori(0, NCH) as it:
                    cols = bass.ds(it * CH, CH)

                    def project(dst, m, c0, c1):
                        n = 0
                        for k in range(KD):
                            for w, xx in ((wh, xTh), (wl, xTh), (wh, xTl)):
                                mm = pe.matmul(dst, w[m][:, k, c0:c1], xx[:, k, cols], start=n == 0, stop=n == 3 * KD - 1)
                                n += 1
                        return mm

                    pe.wait_ge(tl.xl_ready, before(it + tl.turn0))
                    project(psM[0:LAT], "bkv", 0, LAT).then_inc(lat_ready, 1)
                    for g in range(KD):
                        mm = project(bank[0][:, g], "bq", g * P, (g + 1) * P)
                    mm.then_inc(q_ready, 1)
                    pe.wait_ge(latl_done, now(it))
                    for g in range(KD):
                        for n, (w, z) in enumerate(((wh, lath), (wl, lath), (wh, latl))):
                            mm = pe.matmul(bank[1][:, g], w["bk"][:, g * P:(g + 1) * P], z[:], start=n == 0, stop=n == 2)
                    mm.then_inc(k_ready, 1)
                    for j in range(TPC):
                        for n, (w, z) in enumerate(((wh, lath), (wl, lath), (wh, latl))):
                            mm = pe.matmul(psT[:, j // 2, (j % 2) * D:(j % 2 + 1) * D], z[:, j * P:(j + 1) * P],
                                           w["bv"][:], start=n == 0, stop=n == 2)
                    mm.then_inc(v_ready, 1)
                    pe.wait_ge(stacked, (it + 1) * NS)
                    pe.wait_ge(kl_done, now(it))
                    pe.wait_ge(ql_done, now(it))
                    pe.wait_ge(v_done, now(it))
                    for s in range(STEPS):
                        if s < NPAIR:
                            b = s // PPB
                            pe.wait_ge(m_done, now(it, s - 1, NPAIR))
                            for i in range(2):
                                h = 2 * (s % PPB) + i
                                g, half, j = h // HG, (h % HG) // 4, h % 4
                                rows = slice(64 * half, 64 * half + STK)
                                dst = psS[2 * (s % 2) + i]
                                q = QS[rows, 4 * g + j, b * P:(b + 1) * P]
                                pe.matmul(dst[:, 0:PERSIST], q, KS[rows, 4 * g + j, 0:PERSIST], start=True, stop=True)
                                mm = pe.matmul(dst[:, PERSIST:WIN], q,
                                               KS[rows, 4 * g + j, PERSIST + b * P:PERSIST + (b + 2) * P],
                                               start=True, stop=True)
                            mm.then_inc(s_ready, 1)
                        p = s - 2
                        if 0 <= p < NPAIR:
                            b = p // PPB
                            pe.wait_ge(e_done, now(it, 2 * p + 2, 2 * NPAIR))
                            if p % 2 == 0:
                                pe.wait_ge(tv_out, now(it, p // 2, NPAIR // 2))
                            else:
                                pe.wait_ge(ta_out, now(it, p // 2, NPAIR // 2))
                            for i in range(2):
                                for c in range(2):
                                    mm = pe.transpose(psT[:, p % 2, (2 * i + c) * P:(2 * i + c + 1) * P],
                                                      prob[:, 2 * (p % 4) + i,
                                                           PERSIST + c * P:PERSIST + (c + 1) * P], ident[:])
                            mm.then_inc(t_ready, 1)
                            if ends_block(p):
                                pe.wait_ge(pp_done, now(it, p + 1, NPAIR))
                                pe.wait_ge(ol_done, now(it, b, TPC))
                                if b == 0:
                                    pe.wait_ge(tl.xl_ready, before(it + tl.turn0))
                                for g in range(2):
                                    mm = pe.transpose(psM[:, g * P:(g + 1) * P],
                                                      pp[:, b % 2, g * HG:(g + 1) * HG], ident[:])
                                mm.then_inc(pt_ready, 1)
                        p = s - 3
                        if 0 <= p < NPAIR:
                            b = p // PPB
                            if p % 2 == 0:
                                pe.wait_ge(tv_out, now(it, p // 2 + 1, NPAIR // 2))
                            else:
                                pe.wait_ge(ta_out, now(it, p // 2 + 1, NPAIR // 2))
                            if p % PPB == 0:
                                pe.wait_ge(on_done, now(it, b, TPC))
                            for i in range(2):
                                h = 2 * (p % PPB) + i
                                for c in range(2):
                                    mm = pe.matmul(psO[:, (b % 2) * D + h * HD:(b % 2) * D + (h + 1) * HD],
                                                   pT[:, p % 2, (2 * i + c) * P:(2 * i + c + 1) * P],
                                                   V[:, b + c, h * HD:(h + 1) * HD],
                                                   start=h == 0 and c == 0, stop=False, skip_group_check=True)
                            mm.then_inc(pv_done, 1)
                            if ends_block(p):
                                pe.wait_ge(pp_out, now(it, b + 1, TPC))
                                for g in range(2):
                                    mm = pe.matmul(psO[:, (b % 2) * D + g * P:(b % 2) * D + (g + 1) * P],
                                                   ppT[:, g * P:(g + 1) * P], VP[:, g], start=False, stop=True,
                                                   skip_group_check=True)
                                mm.then_inc(o_ready, 1)
                        p = s - 5
                        if ends_block(p):
                            b = p // PPB
                            pe.wait_ge(on_done, now(it, b + 1, TPC))
                            for k in range(KD):
                                mm = pe.transpose(psM[:, (2 + k) * P:(3 + k) * P], on[:, k * P:(k + 1) * P], ident[:])
                            mm.then_inc(oT_ready, 1)
                    pe.wait_ge(ol_done, now(it, TPC, TPC))
                    for i in range(TPC):
                        n = 0
                        for k in range(KD):
                            for oo, w in ((oTh, wh), (oTl, wh), (oTh, wl)):
                                mm = pe.matmul(yT[:, i * D:(i + 1) * D], oo[:, k, i * P:(i + 1) * P], w["bo"][:, k],
                                               start=n == 0, stop=n == 3 * KD - 1)
                                n += 1
                    mm.then_inc(tl.y_ready, 1)
                    tail_pe(pe, tl, it)

            @block.sync
            def _(sp):
                with sp.Fori(0, NCH) as it:
                    sp.wait_ge(s_ready, before(it, NPAIR, NPAIR))
                    stand(sp)
                    sp.wait_ge(halo_done, now(it))
                    stand(sp)
                    for stk, first, done, parts, off in ((QS, (qh, ql), ql_done, (0, 1, 0), 0),
                                                         (KS, (kh, kl), kl_done, (0, 0, 1), PERSIST + P)):
                        sp.wait_ge(done, now(it))
                        stand(sp)
                        for g in range(KD):
                            for half in range(2):
                                for blk in range(3):
                                    src = first[parts[blk]][64 * half:64 * half + 64, g, :]
                                    sp.dma_start(stk[64 * half + HD * blk:64 * half + HD * blk + HD,
                                                     4 * g:4 * g + 4, off:off + CH].bitcast(F32),
                                                 src.bitcast(F32))\
                                      .then_inc(stacked, 16)

            @block.gpsimd
            def _(pool):
                credit(pool, (halo_done, 1), (vhalo_done, 1), (pp_done, NPAIR))
                with pool.Fori(0, NCH) as it:
                    pool.wait_ge(s_ready, before(it, NPAIR, NPAIR))
                    stand(pool)
                    pool.tensor_copy(KS[:, :, PERSIST:PERSIST + P], KS[:, :, PERSIST + CH:KC]).then_inc(halo_done, 1)
                    pool.wait_ge(pv_done, before(it, NPAIR, NPAIR))
                    stand(pool)
                    pool.tensor_copy(V[:, 0], V[:, TPC]).then_inc(vhalo_done, 1)
                    for s in range(NPAIR):
                        b = s // PPB
                        pool.wait_ge(e_done, now(it, 2 * s + 2, 2 * NPAIR))
                        if s % PPB == 0:
                            pool.wait_ge(pt_ready, now(it, b - 1, TPC))
                        h = 2 * (s % PPB)
                        stand(pool)
                        pool.tensor_copy(pp[:, b % 2, h:h + 2], prob[:, 2 * (s % 4):2 * (s % 4) + 2, 0:PERSIST])\
                            .then_inc(pp_done, 1)
                    tail_pool(pool, tl, it)

            @block.scalar
            def _(act):
                credit(act, (lath_done, 1), (qh_done, 1), (kh_done, 1), (v_done, 1), (e_done, 2 * NPAIR),
                       (ta_out, NPAIR // 2), (oh_done, TPC))
                with act.Fori(0, NCH) as it:
                    act.wait_ge(lat_ready, now(it))
                    act.activation(lath[:], psM[0:LAT], ACT.Copy).then_inc(lath_done, 1)
                    act.wait_ge(q_ready, now(it))
                    act.wait_ge(tl.y_ready, before(it + tl.turn0))
                    act.activation(qh[:], bank[0][:], ACT.Copy).then_inc(qh_done, 1)
                    act.wait_ge(k_ready, now(it))
                    act.activation(kh[:], bank[1][:], ACT.Copy).then_inc(kh_done, 1)
                    act.wait_ge(v_ready, now(it))
                    act.wait_ge(vhalo_done, now(it))
                    act.activation(V[:, 1:TPC + 1].rearrange("p a b -> p (a b)"),
                                   psT[:].rearrange("p a b -> p (a b)"), ACT.Copy).then_inc(v_done, 1)
                    for s in range(STEPS):
                        if s < NPAIR:
                            b = s // PPB
                            act.wait_ge(n_done, now(it, s + 1, NPAIR))
                            act.wait_ge(t_ready, now(it, s - 3, NPAIR))
                            act.wait_ge(pp_done, now(it, s - 3, NPAIR))
                            if s % PPB == 0:
                                act.wait_ge(ri_done, now(it, b - 1, TPC))
                            for i in range(2):
                                h = 2 * (s % PPB) + i
                                m = (2 * s + i) % 4
                                act.activation(prob[:, 2 * (s % 4) + i], sm[:, m], ACT.Exp, bias=nmx[:, m:m + 1], scale=SCALE,
                                               accum_out=rs[:, b % 2, h:h + 1]).then_inc(e_done, 1)
                        p = s - 2
                        if 0 <= p < NPAIR and p % 2 == 1:
                            act.wait_ge(t_ready, now(it, p + 1, NPAIR))
                            act.wait_ge(pv_done, now(it, p - 1, NPAIR))
                            act.activation(pT[:, 1], psT[:, 1], ACT.Copy).then_inc(ta_out, 1)
                        p = s - 5
                        if ends_block(p):
                            b = p // PPB
                            act.wait_ge(oT_ready, now(it, b + 1, TPC))
                            if b == 0:
                                act.wait_ge(tl.y_ready, before(it + tl.turn0))
                            act.activation(oTh[:, :, b * P:(b + 1) * P],
                                           psM[:, 2 * P:4 * P].rearrange("p (k c) -> p k c", k=KD), ACT.Copy)\
                               .then_inc(oh_done, 1)
                    tail_act(act, tl, it)

            @block.vector
            def _(dve):
                credit(dve, (latl_done, 1), (ql_done, 1), (kl_done, 1), (m_done, NPAIR), (n_done, NPAIR),
                       (tv_out, NPAIR // 2), (pp_out, TPC), (ri_done, TPC), (on_done, TPC), (ol_done, TPC),
                       (mask_done, 1))
                with dve.Fori(0, NCH) as it:
                    dve.wait_ge(lath_done, now(it))
                    dve.tensor_tensor(latl[:], psM[0:LAT], lath[:].bitcast(F32), ALU.subtract).then_inc(latl_done, 1)
                    dve.wait_ge(qh_done, now(it))
                    dve.tensor_tensor(ql[:], bank[0][:], qh[:].bitcast(F32), ALU.subtract).then_inc(ql_done, 1)
                    dve.wait_ge(kh_done, now(it))
                    dve.tensor_tensor(kl[:], bank[1][:], kh[:].bitcast(F32), ALU.subtract).then_inc(kl_done, 1)
                    dve.wait_ge(mask_done, before(it))
                    for s in range(STEPS):
                        if s < NPAIR:
                            b = s // PPB
                            dve.wait_ge(s_ready, now(it, s + 1, NPAIR))
                            dve.wait_ge(e_done, now(it, 2 * s - 2, 2 * NPAIR))
                            stand(dve)
                            for i in range(2):
                                m = (2 * s + i) % 4
                                ins = dve.tensor_tensor_reduce(sm[:, m], psS[m][:, 0:WIN], masks[:, b], 1.0, -3.0e38,
                                                               ALU.add, ALU.max, mx[:, m:m + 1])
                            ins.then_inc(m_done, 1)
                            dve.wait_ge(m_done, now(it, s + 1, NPAIR))
                            m = (2 * s) % 4
                            dve.tensor_scalar(nmx[:, m:m + 2], mx[:, m:m + 2], -SCALE, None, ALU.mult).then_inc(n_done, 1)
                        p = s - 2
                        if 0 <= p < NPAIR and p % 2 == 0:
                            dve.wait_ge(t_ready, now(it, p + 1, NPAIR))
                            dve.wait_ge(pv_done, now(it, p - 1, NPAIR))
                            dve.tensor_copy(pT[:, 0], psT[:, 0]).then_inc(tv_out, 1)
                        if ends_block(p):
                            b = p // PPB
                            dve.wait_ge(pt_ready, now(it, b + 1, TPC))
                            dve.wait_ge(o_ready, now(it, b, TPC))
                            dve.tensor_copy(ppT[:], psM[:, 0:2 * P]).then_inc(pp_out, 1)
                            dve.reciprocal(rinv[:], rs[:, b % 2]).then_inc(ri_done, 1)
                        p = s - 3
                        if ends_block(p):
                            b = p // PPB
                            dve.wait_ge(o_ready, now(it, b + 1, TPC))
                            dve.wait_ge(ri_done, now(it, b + 1, TPC))
                            dve.wait_ge(oT_ready, now(it, b, TPC))
                            dve.tensor_tensor(on[:].rearrange("p (h d) -> p h d", d=HD),
                                              psO[:, (b % 2) * D:(b % 2 + 1) * D].rearrange("p (h d) -> p h d", d=HD),
                                              rinv[:].unsqueeze(2).broadcast_to([P, HB, HD]), ALU.mult).then_inc(on_done, 1)
                        p = s - 5
                        if ends_block(p):
                            b = p // PPB
                            dve.wait_ge(oh_done, now(it, b + 1, TPC))
                            dve.tensor_tensor(oTl[:, :, b * P:(b + 1) * P],
                                              psM[:, 2 * P:4 * P].rearrange("p (k c) -> p k c", k=KD),
                                              oTh[:, :, b * P:(b + 1) * P].bitcast(F32), ALU.subtract).then_inc(ol_done, 1)
                    dve.tensor_copy(masks[:, 0:2], masks[:, 2:4]).then_inc(mask_done, 1)
                    tail_norm_dve(dve, tl, it, add=True)
                    tail_split_dve(dve, tl, it)


def attention_inputs(a):
    g = lambda n: np.asarray(a["L0_attn_b_" + n])
    r, c = np.arange(P)[:, None], np.arange(P)[None, :]
    ok = np.zeros((P, 4, WIN), bool)
    for i in range(4):
        ok[:, i, PERSIST + P:] = c <= r
        if i > 0:
            ok[:, i, PERSIST:PERSIST + P] = c > r
            ok[:, i, 0:PERSIST] = (c <= r)[:, 0:PERSIST] if i == 1 else True
    order = np.arange(D).reshape(D // 64, 4, HD).transpose(0, 2, 1).reshape(-1)
    return {"bq": g("Wq")[:, order], "bkv": g("Wkv"), "bk": g("Wk")[:, order], "bv": g("Wv"), "bo": g("Wo"),
            "masks": np.where(ok, 0.0, MASKED).astype(np.float32)}


def kernel(**inputs):
    import concourse.bacc as bacc
    from concourse.bass_utils import run_bass_kernel_spmd

    nc = bacc.Bacc("TRN2", target_bir_lowering=False, num_devices=1)
    arrays = {f"in_{n}": np.ascontiguousarray(v) for n, v in host_inputs(inputs).items()}
    t = {n[3:]: nc.dram_tensor(n, v.shape, mybir.dt.from_np(v.dtype), kind="ExternalInput").ap()
         for n, v in arrays.items()}
    out = nc.dram_tensor("out_dram", (T, D), F32, kind="ExternalOutput").ap()
    build(nc, t, out)
    r = run_bass_kernel_spmd(nc, [arrays], core_ids=[0])
    return r.results[0]["out_dram"].reshape(1, T, D)
```

```python
from contextlib import ExitStack

import numpy as np

import concourse.bass as bass
from concourse import mybir

P = 128
F32 = mybir.dt.float32
F32R = mybir.dt.float32r
ALU = mybir.AluOpType
ACT = mybir.ActivationFunctionType
AX = mybir.AxisListType

T, D = 2048, 256
KD = D // P
CH = 512
NCH = T // CH
TPC = CH // P
PAD = 4
EPS = 1e-5

HA, HV, TAPS = 6, 64, 4
UNITS = 2
VT, GT = 4, 3

NE, FH = 8, 176
FT = NE * FH // P

HB, HD = 16, 16
LAT = 64
PERSIST = 16
WIN = PERSIST + 2 * P
HG = HB // 2
STK = 3 * HD
MASKED = -1e30

MAGIC = 12582912.0
TWO_PI = 6.283185


def now(it, k=1, n=1):
    return (it + 1) * n + k


def before(it, k=1, n=1):
    return it * n + k


def build(nc, t, out, stop=4):
    ctx = ExitStack()
    with ctx:
        def sb(name, shape, dt=F32):
            return ctx.enter_context(nc.sbuf_tensor(name, shape, dt))

        def sem(name):
            return ctx.enter_context(nc.semaphore(name))

        x = sb("x_tok", [P, T // P * D])
        xTh = sb("xTh", [P, KD, PAD + T], F32R)
        xTl = sb("xTl", [P, KD, PAD + T], F32R)
        xn = sb("xn", [P, TPC, D])
        stats = sb("stats", [P, TPC, 6])
        meanvar = sb("meanvar", [P, TPC, 2])
        rstd = sb("rstd", [P, TPC])
        vareps = sb("vareps", [P, TPC])
        minus_half = sb("minus_half", [P, 32])
        ident = sb("ident_sb", [P, P])

        bank = [ctx.enter_context(nc.psum_tensor(f"bank{i}", [P, 2, CH], F32)) for i in range(4)]
        psY = bank[3]
        yT = psY[:].rearrange("p a b -> p (a b)")

        consts_in = sem("consts_in")
        x_chunk = [sem(f"x_chunk{c}") for c in range(NCH)]

        def xcols(it, t0=0, n=TPC):
            return x[:, bass.ds(it * (TPC * D) + t0 * D, n * D)]

        class Tail:

            def __init__(self, ph, base=0):
                self.turn0 = 0
                self.base = base
                self.y_ready = sem(f"y_ready{ph}")
                self.x_new = sem(f"x_new{ph}")
                self.stat_ready = sem(f"stat{ph}")
                self.mv_ready = sem(f"mv{ph}")
                self.vareps_ready = sem(f"vareps{ph}")
                self.rstd_ready = sem(f"rstd{ph}")
                self.xn_ready = sem(f"xn{ph}")
                self.xT_ready = sem(f"xT{ph}")
                self.xh_ready = sem(f"xh{ph}")
                self.xl_ready = sem(f"xl{ph}")

        passed = sem("passed")

        def stand(eng):
            eng.sem_inc(passed, 1)

        def credit(eng, *sems):
            for s, n in sems:
                eng.sem_inc(s, n)

        def tail_norm_dve(dve, tl, it, add):
            if add:
                dve.wait_ge(tl.y_ready, now(it + tl.turn0))
                dve.tensor_tensor(xcols(it), yT, xcols(it), ALU.add).then_inc(tl.x_new, 1)
                dve.wait_ge(tl.x_new, now(it + tl.turn0))
            stand(dve)
            for i in range(TPC):
                dve.bn_stats(stats[:, i, :], xcols(it, i, 1)).then_inc(tl.stat_ready, 1)
            dve.wait_ge(tl.stat_ready, now(it + tl.turn0, TPC, TPC))
            stand(dve)
            for i in range(TPC):
                dve.bn_aggr(meanvar[:, i, :], stats[:, i, :]).then_inc(tl.mv_ready, 1)
            dve.wait_ge(tl.mv_ready, now(it + tl.turn0, TPC, TPC))
            dve.wait_ge(tl.rstd_ready, now(it + tl.turn0))
            dve.wait_ge(tl.xT_ready, before(it + tl.turn0))
            for i in range(TPC):
                dve.tensor_scalar(xn[:, i, :], xcols(it, i, 1), meanvar[:, i, 0:1], rstd[:, i:i + 1],
                                  ALU.subtract, ALU.mult).then_inc(tl.xn_ready, 1)

        def tail_split_dve(dve, tl, it):
            dve.wait_ge(tl.xh_ready, now(it + tl.turn0))
            dve.tensor_tensor(xTl[:, :, bass.ds(it * CH + tl.base, CH)], psY[:],
                              xTh[:, :, bass.ds(it * CH + tl.base, CH)].bitcast(F32),
                              ALU.subtract).then_inc(tl.xl_ready, 1)

        def tail_pool(pool, tl, it):
            pool.wait_ge(tl.mv_ready, now(it + tl.turn0, TPC, TPC))
            pool.wait_ge(tl.xn_ready, before(it + tl.turn0, TPC, TPC))
            stand(pool)
            pool.tensor_scalar(vareps[:], meanvar[:, :, 1], EPS, None, ALU.add).then_inc(tl.vareps_ready, 1)
            pool.wait_ge(tl.vareps_ready, now(it + tl.turn0))
            pool.tensor_tensor(rstd[:], vareps[:], minus_half[:, 0:TPC], ALU.pow).then_inc(tl.rstd_ready, 1)

        def tail_pe(pe, tl, it):
            pe.wait_ge(tl.xn_ready, now(it + tl.turn0, TPC, TPC))
            for k in range(KD):
                for i in range(TPC):
                    last = pe.transpose(psY[:, k, i * P:(i + 1) * P], xn[:, i, k * P:(k + 1) * P], ident[:])
            last.then_inc(tl.xT_ready, 1)

        def tail_act(act, tl, it):
            act.wait_ge(tl.xT_ready, now(it + tl.turn0))
            act.activation(xTh[:, :, bass.ds(it * CH + tl.base, CH)], psY[:], ACT.Copy).then_inc(tl.xh_ready, 1)

        t0 = Tail(0, base=PAD)
        zero_pad = sem("zero_pad")
        half_set = sem("half_set")
        padf = sb("padf", [P, KD * PAD])
        rec_ctx, prep = ExitStack(), ExitStack()
        rec_wts, rec_load, rec_split_dve, rec_split_pool = recurrence_weights(nc, rec_ctx, prep, t, sem)
        with nc.Block() as block:
            @block.sync
            def _(sp):
                sp.dma_start(ident[:], t["ident"]).then_inc(consts_in, 16)
                for c in range(NCH):
                    tiles = slice(c * TPC, (c + 1) * TPC)
                    sp.dma_start(x[:].rearrange("p (t d) -> p t d", d=D)[:, tiles],
                                 t["x"].rearrange("(t p) d -> p t d", p=P)[:, tiles]).then_inc(x_chunk[c], 16)
                rec_load(sp)

            @block.gpsimd
            def _(pool):
                credit(pool, (t0.rstd_ready, 1), (t0.vareps_ready, 1))
                pool.memset(minus_half[:], -0.5).then_inc(half_set, 1)
                pool.wait_ge(half_set, 1)
                with pool.Fori(0, NCH) as it:
                    tail_pool(pool, t0, it)
                rec_split_pool(pool)

            @block.vector
            def _(dve):
                credit(dve, (t0.stat_ready, TPC), (t0.mv_ready, TPC), (t0.xn_ready, TPC), (t0.xl_ready, 1))
                dve.memset(padf[:], 0.0).then_inc(zero_pad, 1)
                dve.wait_ge(zero_pad, 1)
                for w in (xTh, xTl):
                    dve.tensor_copy(w[:, :, 0:PAD], padf[:].rearrange("p (k c) -> p k c", k=KD))\
                       .then_inc(zero_pad, 1)
                for c in range(NCH + 1):
                    if c < NCH:
                        dve.wait_ge(x_chunk[c], 16)
                        tail_norm_dve(dve, t0, c, add=False)
                    if c > 0:
                        tail_split_dve(dve, t0, c - 1)
                rec_split_dve(dve)

            @block.tensor
            def _(pe):
                credit(pe, (t0.xT_ready, 1))
                pe.wait_ge(consts_in, 16)
                with pe.Fori(0, NCH) as it:
                    pe.wait_ge(t0.xl_ready, before(it))
                    tail_pe(pe, t0, it)

            @block.scalar
            def _(act):
                credit(act, (t0.xh_ready, 1))
                with act.Fori(0, NCH) as it:
                    tail_act(act, t0, it)
        prep.close()

        tl = Tail("N")
        if stop > 0:
            recurrence(nc, ctx, rec_ctx, rec_wts, x, xTh, xTl, yT, psY, bank, tl, stand, credit, tail_norm_dve, tail_split_dve,
                       tail_pool, tail_pe, tail_act, sem, ident, minus_half)
        wts = ffn_weights(nc, ctx, t, sem) if stop > 1 else None
        ffn_sems = {}

        def tail_after(phases):
            tl.turn0 = phases * NCH
            return tl

        if stop > 1:
            experts(nc, t, wts, x, xTh, xTl, yT, psY, bank, tail_after(1), stand, credit, tail_norm_dve, tail_split_dve,
                    tail_pool, tail_pe, tail_act, sem, ident, xcols, ffn_sems, last=False)
        if stop > 2:
            attention(nc, t, x, xTh, xTl, yT, psY, bank, tail_after(2), stand, credit, tail_norm_dve, tail_split_dve,
                      tail_pool, tail_pe, tail_act, sem, ident)
        stored = sem("stored")
        if stop > 3:
            experts(nc, t, wts, x, xTh, xTl, yT, psY, bank, tail_after(3), stand, credit, tail_norm_dve, tail_split_dve,
                    tail_pool, tail_pe, tail_act, sem, ident, xcols, ffn_sems, last=True, out=out, stored=stored)


def heads_of_tile(u):
    return [p // 32 if u == 0 else 4 + (p % 64) // 32 for p in range(P)]


def recurrence_weights(nc, ctx, prep, t, sem):
    def sb(name, shape, dt=F32):
        return ctx.enter_context(nc.sbuf_tensor(name, shape, dt))

    wfh, wfl = sb("wfh", [P, KD, TAPS, 2 * P], F32R), sb("wfl", [P, KD, TAPS, 2 * P], F32R)
    wvh, wvl = sb("wvh", [P, KD, VT * P], F32R), sb("wvl", [P, KD, VT * P], F32R)
    wgh, wgl = sb("wgh", [P, KD, GT * P], F32R), sb("wgl", [P, KD, GT * P], F32R)
    woh, wol = sb("woh", [P, GT, D], F32R), sb("wol", [P, GT, D], F32R)
    wabh, wabl = sb("wabh", [P, KD, 2 * HA], F32R), sb("wabl", [P, KD, 2 * HA], F32R)
    sel = sb("sel", [2 * HA, 4, P], F32R)
    selr = sb("selr", [8, 2, P], F32R)
    headsum = sb("headsum", [P, 2, 8])
    convv = sb("convv", [P, VT, TAPS])
    rmsw = sb("rmsw", [P, GT])
    sscale = sb("sscale", [P, 2])

    def pb(name, shape, dt=F32):
        return prep.enter_context(nc.sbuf_tensor(name, shape, dt))

    wq_raw, wk_raw = pb("wq_raw", [P, KD, 2 * P]), pb("wk_raw", [P, KD, 2 * P])
    cq_raw, ck_raw = pb("cq_raw", [P, TAPS, 2 * P]), pb("ck_raw", [P, TAPS, 2 * P])
    freq = pb("freq", [P, 2 * P])
    wv_raw, wg_raw = pb("wv_raw", [P, KD, VT * P]), pb("wg_raw", [P, KD, GT * P])
    wo_raw, wab_raw = pb("wo_raw", [P, GT, D]), pb("wab_raw", [P, KD, 2 * HA])
    sel_raw, selr_raw = pb("sel_raw", [2 * HA, 4, P]), pb("selr_raw", [8, 2, P])
    kq, qq = pb("kq", [P, KD, TAPS, 2 * P]), pb("qq", [P, KD, TAPS, 2 * P])

    a_in = sem("a_in")
    prep_dve = sem("prep_dve")
    prep_pool = sem("prep_pool")
    loads = [(wk_raw[:], t["wk"].rearrange("(k p) m -> p k m", p=P)),
             (ck_raw[:], t["ck"].rearrange("(o j) m -> o j m", o=1).broadcast_to([P, TAPS, 2 * P])),
             (freq[:], t["freq"].broadcast_to([P, 2 * P])),
             (wq_raw[:], t["wq"].rearrange("(k p) m -> p k m", p=P)),
             (cq_raw[:], t["cq"].rearrange("(o j) m -> o j m", o=1).broadcast_to([P, TAPS, 2 * P])),
             (wv_raw[:], t["wv"].rearrange("(k p) m -> p k m", p=P)),
             (wg_raw[:], t["wg"].rearrange("(k p) m -> p k m", p=P)),
             (wo_raw[:], t["wo"].rearrange("(k p) m -> p k m", p=P)),
             (wab_raw[:], t["wab"].rearrange("(k p) m -> p k m", p=P)),
             (sel_raw[:], t["sel"]), (selr_raw[:], t["selr"]),
             (headsum[:], t["headsum"]), (convv[:], t["convv"]), (rmsw[:], t["rmsw"]),
             (sscale[:], t["sscale"])]

    def load(sp):
        for dst, src in loads:
            sp.dma_start(dst, src).then_inc(a_in, 16)

    def split_dve(dve):
        n = 0

        def link(ins):
            nonlocal n
            n += 1
            ins.then_inc(prep_dve, 1)
            dve.wait_ge(prep_dve, n)
        dve.wait_ge(a_in, 16 * len(loads))
        link(dve.tensor_tensor(ck_raw[:], ck_raw[:], freq[:].unsqueeze(1).broadcast_to([P, TAPS, 2 * P]), ALU.mult))
        for k in range(KD):
            link(dve.tensor_tensor(kq[:, k], ck_raw[:], wk_raw[:, k].unsqueeze(1).broadcast_to([P, TAPS, 2 * P]), ALU.mult))
        link(dve.tensor_copy(sel[:], sel_raw[:]))
        link(dve.tensor_copy(selr[:], selr_raw[:]))
        for h, l, raw in ((wvh, wvl, wv_raw), (wabh, wabl, wab_raw)):
            link(dve.tensor_copy(h[:], raw[:]))
            link(dve.tensor_tensor(l[:], raw[:], h[:].bitcast(F32), ALU.subtract))
        dve.wait_ge(prep_pool, 1)
        link(dve.tensor_tensor(qq[:, KD - 1], cq_raw[:], wq_raw[:, KD - 1].unsqueeze(1).broadcast_to([P, TAPS, 2 * P]), ALU.mult))
        dve.wait_ge(prep_pool, KD)
        link(dve.tensor_tensor(kq[:], kq[:], qq[:], ALU.subtract))
        link(dve.tensor_copy(wfh[:], kq[:]))
        link(dve.tensor_tensor(wfl[:], kq[:], wfh[:].bitcast(F32), ALU.subtract))

    def split_pool(pool):
        n = 0

        def link(ins):
            nonlocal n
            n += 1
            ins.then_inc(prep_pool, 1)
            pool.wait_ge(prep_pool, n)
        pool.wait_ge(a_in, 16 * len(loads))
        link(pool.tensor_tensor(cq_raw[:], cq_raw[:], freq[:].unsqueeze(1).broadcast_to([P, TAPS, 2 * P]), ALU.mult))
        for k in range(KD - 1):
            link(pool.tensor_tensor(qq[:, k], cq_raw[:], wq_raw[:, k].unsqueeze(1).broadcast_to([P, TAPS, 2 * P]), ALU.mult))
        for h, l, raw in ((wgh, wgl, wg_raw), (woh, wol, wo_raw)):
            link(pool.tensor_copy(h[:], raw[:]))
            link(pool.tensor_tensor(l[:], raw[:], h[:].bitcast(F32), ALU.subtract))
    wts = (wfh, wfl, wvh, wvl, wgh, wgl, woh, wol, wabh, wabl, sel, selr, headsum, convv, rmsw, sscale)
    return wts, load, split_dve, split_pool


def recurrence(nc, octx, ctx, wts, x, xTh, xTl, yT, psY, bank, tl, stand, credit, tail_norm_dve, tail_split_dve,
               tail_pool, tail_pe, tail_act, osem, ident, minus_half):
    wfh, wfl, wvh, wvl, wgh, wgl, woh, wol, wabh, wabl, sel, selr, headsum, convv, rmsw, sscale = wts
    with ctx:
        def sb(name, shape, dt=F32):
            return ctx.enter_context(nc.sbuf_tensor(name, shape, dt))

        sem = osem
        whole = sb("whole", [P, 2, CH])
        angle = sb("angle", [P, 2, CH])
        vraw = sb("vraw", [P, VT, PAD + CH])
        vconv = sb("vconv", [P, VT, CH])
        w = sb("w", [P, GT, CH])
        o = sb("o", [P, GT, CH])
        gate = sb("gate", [P, GT, CH])
        sq = sb("sq", [P, GT, CH])
        oh, ol = sb("oh", [P, GT, CH], F32R), sb("ol", [P, GT, CH], F32R)
        carry = sb("carry", [P, GT])
        sg = sb("sg", [2 * HA, CH])
        sgh, sgl = sb("sgh", [2 * HA, CH], F32R), sb("sgl", [2 * HA, CH], F32R)
        ms = sb("ms", [P, TPC * HA])
        rms = sb("rms", [P, TPC * HA])
        rmsh, rmsl = sb("rmsh", [HA, CH], F32R), sb("rmsl", [HA, CH], F32R)

        psF, psV, psB = bank[0], bank[1], bank[2]
        f_ready = sem("f_ready")
        ab_ready = sem("ab_ready")
        vg_ready = sem("vg_ready")
        beta_ready = sem("beta_ready")
        alpha_ready = sem("alpha_ready")
        ss_ready = sem("ss_ready")
        rT_ready = sem("rT_ready")
        rb_ready = sem("rb_ready")
        sg_ready = sem("sg_ready")
        vg_out = sem("vg_out")
        abs_ready = sem("abs_ready")
        cos_ready = sem("cos_ready")
        sin_ready = sem("sin_ready")
        sq_ready = sem("sq_ready")
        zeroed = sem("zeroed")
        sgh_ready = sem("sgh_ready")
        sgl_ready = sem("sgl_ready")
        whole_ready = sem("whole_ready")
        angle_ready = sem("angle_ready")
        tap_done = sem("tap_done")
        halo_done = sem("halo_done")
        rot_done = sem("rot_done")
        scan_done = sem("scan_done")
        carry_done = sem("carry_done")
        gated = sem("gated")
        ms_ready = sem("ms_ready")
        rms_ready = sem("rms_ready")
        rh_ready = sem("rh_ready")
        rl_ready = sem("rl_ready")
        o2_ready = sem("o2_ready")
        oh_ready = sem("oh_ready")
        ol_ready = sem("ol_ready")
        NVG = VT + GT
        NTAP = VT * TAPS
        NROT = 8

        with nc.Block() as block:
            @block.tensor
            def _(pe):
                credit(pe, (vg_ready, NVG), (f_ready, 1), (ab_ready, 1), (beta_ready, 1), (alpha_ready, 1),
                       (ss_ready, 1), (rT_ready, 1), (rb_ready, 1), (tl.y_ready, 1), (tl.xT_ready, 1))
                def angles(it):
                    for u in range(UNITS):
                        n = 0
                        for j in range(TAPS):
                            for k in range(KD):
                                cols = bass.ds(it * CH + PAD - TAPS + 1 + j, CH)
                                for wt, xx in ((wfh, xTh), (wfl, xTh), (wfh, xTl)):
                                    last = pe.matmul(psV[:, u], wt[:, k, j, u * P:(u + 1) * P], xx[:, k, cols],
                                                     start=n == 0, stop=n == 3 * KD * TAPS - 1)
                                    n += 1
                    last.then_inc(f_ready, 1)

                def project(it, dst, wh, wl, c0, c1):
                    n = 0
                    for k in range(KD):
                        cols = bass.ds(it * CH + PAD, CH)
                        for wt, xx in ((wh, xTh), (wl, xTh), (wh, xTl)):
                            last = pe.matmul(dst, wt[:, k, c0:c1], xx[:, k, cols],
                                             start=n == 0, stop=n == 3 * KD - 1)
                            n += 1
                    return last

                def value_or_gate(it, i):
                    pe.wait_ge(vg_out, now(it, i - 1, NVG))
                    if i == 0:
                        pe.wait_ge(angle_ready, now(it))
                    if i < VT:
                        mm = project(it, psV[:, i % 2], wvh, wvl, i * P, (i + 1) * P)
                    else:
                        mm = project(it, psV[:, i % 2], wgh, wgl, (i - VT) * P, (i - VT + 1) * P)
                    mm.then_inc(vg_ready, 1)

                def start(it):
                    pe.wait_ge(rl_ready, before(it))
                    stand(pe)
                    project(it, psB[0:2 * HA, 0], wabh, wabl, 0, 2 * HA).then_inc(ab_ready, 1)
                    for i in range(2):
                        value_or_gate(it, i)

                def chunk(it, ahead):
                    for i in range(2, NVG):
                        value_or_gate(it, i)
                        if i == VT - 1:
                            pe.wait_ge(sgl_ready, now(it))
                            for u in range(UNITS):
                                pe.matmul(psB[:, u], sel[:, 2 + u], sgh[:], start=True, stop=False)
                                last = pe.matmul(psB[:, u], sel[:, 2 + u], sgl[:], start=False, stop=True)
                            last.then_inc(beta_ready, 1)
                    pe.wait_ge(o2_ready, before(it, GT, GT))
                    for u in range(UNITS):
                        pe.matmul(psF[:, u], sel[:, u], sgh[:], start=True, stop=False)
                        last = pe.matmul(psF[:, u], sel[:, u], sgl[:], start=False, stop=True)
                    last.then_inc(alpha_ready, 1)
                    if ahead:
                        pe.wait_ge(vg_out, now(it, NVG, NVG))
                        angles(it + 1)
                    for g in range(GT):
                        pe.wait_ge(sq_ready, now(it, g + 1, GT))
                        for i in range(TPC):
                            last = pe.matmul(psB[:, 0, i * HA:(i + 1) * HA], sq[:, g, i * P:(i + 1) * P],
                                             headsum[:, g // 2, 0:HA], start=g == 0 and i == 0, stop=g == GT - 1,
                                             skip_group_check=True)
                    last.then_inc(ss_ready, 1)
                    pe.wait_ge(rms_ready, now(it))
                    for i in range(TPC):
                        last = pe.transpose(psB[0:HA, 1, i * P:(i + 1) * P], rms[:, i * HA:(i + 1) * HA], ident[:])
                    last.then_inc(rT_ready, 1)
                    pe.wait_ge(rl_ready, now(it))
                    for u in range(UNITS):
                        pe.matmul(psF[:, u], selr[0:HA, u], rmsh[:], start=True, stop=False)
                        last = pe.matmul(psF[:, u], selr[0:HA, u], rmsl[:], start=False, stop=True)
                    last.then_inc(rb_ready, 1)
                    pe.wait_ge(ol_ready, now(it))
                    pe.wait_ge(tl.xl_ready, before(it + tl.turn0))
                    for i in range(TPC):
                        n = 0
                        for g in range(GT):
                            for oo, ww in ((oh, woh), (ol, woh), (oh, wol)):
                                last = pe.matmul(yT[:, i * D:(i + 1) * D], oo[:, g, i * P:(i + 1) * P], ww[:, g],
                                                 start=n == 0, stop=n == 3 * GT - 1)
                                n += 1
                    last.then_inc(tl.y_ready, 1)
                    if ahead:
                        start(it + 1)
                    tail_pe(pe, tl, it)

                angles(0)
                start(0)
                with pe.Fori(0, NCH - 1) as it:
                    chunk(it, ahead=True)
                chunk(NCH - 1, ahead=False)

            @block.scalar
            def _(act):
                credit(act, (sg_ready, 1), (vg_out, NVG), (abs_ready, 1), (cos_ready, 1), (sin_ready, 1),
                       (sq_ready, GT), (tl.xh_ready, 1))
                def start(it):
                    act.wait_ge(ab_ready, now(it))
                    act.wait_ge(sgl_ready, before(it))
                    act.activation(sg[:], psB[0:2 * HA, 0], ACT.Sigmoid).then_inc(sg_ready, 1)
                    act.wait_ge(halo_done, before(it))
                    for i in range(2):
                        act.wait_ge(vg_ready, now(it, i + 1, NVG))
                        act.activation(vraw[:, i, PAD:PAD + CH], psV[:, i % 2], ACT.Copy).then_inc(vg_out, 1)

                def chunk(it, ahead):
                    for i in range(2, VT):
                        act.wait_ge(vg_ready, now(it, i + 1, NVG))
                        act.activation(vraw[:, i, PAD:PAD + CH], psV[:, i % 2], ACT.Copy).then_inc(vg_out, 1)
                    act.wait_ge(angle_ready, now(it))
                    act.activation(whole[:], angle[:], ACT.Abs).then_inc(abs_ready, 1)
                    act.wait_ge(abs_ready, now(it))
                    act.activation(whole[:], whole[:], ACT.Sin, bias=sscale[:, 1:2], scale=-TWO_PI)\
                       .then_inc(cos_ready, 1)
                    act.activation(angle[:, 0], angle[:, 0], ACT.Sin, scale=TWO_PI)
                    act.activation(angle[:, 1], angle[:, 1], ACT.Sin, scale=sscale[:, 0:1]).then_inc(sin_ready, 1)
                    act.wait_ge(o2_ready, before(it, GT, GT))
                    for i in range(VT, NVG):
                        act.wait_ge(vg_ready, now(it, i + 1, NVG))
                        act.activation(gate[:, i - VT], psV[:, i % 2], ACT.Silu).then_inc(vg_out, 1)
                    act.wait_ge(ol_ready, before(it))
                    for g in range(GT):
                        act.wait_ge(scan_done, now(it, g + 1, GT))
                        act.activation(sq[:, g], o[:, g], ACT.Square).then_inc(sq_ready, 1)
                    if ahead:
                        start(it + 1)
                    tail_act(act, tl, it)

                start(0)
                with act.Fori(0, NCH - 1) as it:
                    chunk(it, ahead=True)
                chunk(NCH - 1, ahead=False)

            @block.gpsimd
            def _(pool):
                credit(pool, (tl.rstd_ready, 1), (tl.vareps_ready, 1), (rms_ready, 1))
                with pool.Fori(0, NCH) as it:
                    pool.wait_ge(ms_ready, now(it))
                    pool.wait_ge(rT_ready, before(it))
                    pool.tensor_tensor(rms[:], ms[:], minus_half[:, 0:TPC * HA], ALU.pow).then_inc(rms_ready, 1)
                    tail_pool(pool, tl, it)

            @block.vector
            def _(dve):
                credit(dve, (sgh_ready, 1), (sgl_ready, 1), (whole_ready, 1), (angle_ready, 1), (tap_done, NTAP),
                       (halo_done, 1), (rot_done, NROT), (scan_done, GT), (carry_done, 1), (gated, 1), (ms_ready, 1),
                       (rh_ready, 1), (rl_ready, 1), (o2_ready, GT), (oh_ready, 1), (ol_ready, 1), (tl.x_new, 1),
                       (tl.stat_ready, TPC), (tl.mv_ready, TPC), (tl.xn_ready, TPC), (tl.xl_ready, 1))
                dve.memset(vraw[:, :, 0:PAD], 0.0).then_inc(zeroed, 1)
                dve.memset(carry[:], 0.0).then_inc(zeroed, 1)
                dve.wait_ge(zeroed, 2)
                def start(it):
                    dve.wait_ge(f_ready, now(it))
                    dve.tensor_scalar(whole[:], psV[:], MAGIC, -MAGIC, ALU.add, ALU.add).then_inc(whole_ready, 1)
                    dve.wait_ge(whole_ready, now(it))
                    dve.tensor_tensor(angle[:], psV[:], whole[:], ALU.subtract).then_inc(angle_ready, 1)

                def chunk(it, ahead):
                    dve.wait_ge(sg_ready, now(it))
                    dve.wait_ge(alpha_ready, before(it))
                    dve.tensor_copy(sgh[:], sg[:]).then_inc(sgh_ready, 1)
                    dve.wait_ge(sgh_ready, now(it))
                    dve.tensor_tensor(sgl[:], sg[:], sgh[:].bitcast(F32), ALU.subtract).then_inc(sgl_ready, 1)
                    for j in range(TAPS):
                        for i in range(VT):
                            src = vraw[:, i, PAD - TAPS + 1 + j:PAD - TAPS + 1 + j + CH]
                            if j == 0:
                                dve.wait_ge(vg_out, now(it, i + 1, NVG))
                                dve.tensor_scalar(vconv[:, i], src, convv[:, i, 0:1], None, ALU.mult)\
                                   .then_inc(tap_done, 1)
                            else:
                                dve.wait_ge(tap_done, now(it, (j - 1) * VT + i + 1, NTAP))
                                dve.scalar_tensor_tensor(vconv[:, i], src, convv[:, i, j:j + 1], vconv[:, i],
                                                         ALU.mult, ALU.add).then_inc(tap_done, 1)
                    dve.tensor_copy(vraw[:, :, 1:PAD], vraw[:, :, CH + 1:CH + PAD]).then_inc(halo_done, 1)
                    dve.wait_ge(tap_done, now(it, NTAP, NTAP))
                    dve.wait_ge(sin_ready, now(it))
                    cos01 = whole[:, 0].unsqueeze(1).broadcast_to([P, 2, CH])
                    dve.tensor_tensor(o[:, 0:2], vconv[:, 0:2], cos01, ALU.mult).then_inc(rot_done, 1)
                    dve.tensor_tensor(o[:, 2], vconv[:, 2], whole[:, 1], ALU.mult).then_inc(rot_done, 1)
                    dve.tensor_tensor(w[:, 0], vconv[:, 1], angle[:, 0], ALU.mult).then_inc(rot_done, 1)
                    dve.tensor_tensor(w[:, 1], vconv[:, 0], angle[:, 0], ALU.mult).then_inc(rot_done, 1)
                    dve.tensor_tensor(w[:, 2], vconv[:, 3], angle[:, 1], ALU.mult).then_inc(rot_done, 1)
                    dve.wait_ge(rot_done, now(it, 5, NROT))
                    dve.tensor_tensor(w[:, 0], o[:, 0], w[:, 0], ALU.subtract).then_inc(rot_done, 1)
                    dve.tensor_tensor(w[:, 1:3], o[:, 1:3], w[:, 1:3], ALU.add).then_inc(rot_done, 1)
                    dve.wait_ge(rot_done, now(it, 7, NROT))
                    dve.wait_ge(beta_ready, now(it))
                    beta01 = psB[:, 0].unsqueeze(1).broadcast_to([P, 2, CH])
                    dve.tensor_tensor(w[:, 0:2], w[:, 0:2], beta01, ALU.mult)
                    dve.tensor_tensor(w[:, 2], w[:, 2], psB[:, 1], ALU.mult).then_inc(rot_done, 1)
                    dve.wait_ge(rot_done, now(it, 8, NROT))
                    dve.wait_ge(alpha_ready, now(it))
                    dve.wait_ge(carry_done, before(it))
                    for g in range(GT):
                        dve.tensor_tensor_scan(o[:, g], psF[:, g // 2], w[:, g], carry[:, g:g + 1],
                                               ALU.mult, ALU.add).then_inc(scan_done, 1)
                    dve.wait_ge(scan_done, now(it, GT, GT))
                    dve.tensor_copy(carry[:], o[:, :, CH - 1]).then_inc(carry_done, 1)
                    dve.wait_ge(vg_out, now(it, NVG, NVG))
                    dve.tensor_tensor(gate[:], gate[:], o[:], ALU.mult).then_inc(gated, 1)
                    dve.wait_ge(ss_ready, now(it))
                    dve.wait_ge(rms_ready, before(it))
                    dve.tensor_scalar(ms[:], psB[:, 0, 0:TPC * HA], EPS, None, ALU.add).then_inc(ms_ready, 1)
                    dve.wait_ge(rT_ready, now(it))
                    dve.wait_ge(rb_ready, before(it))
                    dve.tensor_copy(rmsh[:], psB[0:HA, 1]).then_inc(rh_ready, 1)
                    dve.wait_ge(rh_ready, now(it))
                    dve.tensor_tensor(rmsl[:], psB[0:HA, 1], rmsh[:].bitcast(F32), ALU.subtract)\
                       .then_inc(rl_ready, 1)
                    dve.wait_ge(rb_ready, now(it))
                    dve.wait_ge(gated, now(it))
                    for g in range(GT):
                        dve.scalar_tensor_tensor(sq[:, g], gate[:, g], rmsw[:, g:g + 1], psF[:, g // 2],
                                                 ALU.mult, ALU.mult).then_inc(o2_ready, 1)
                    dve.wait_ge(o2_ready, now(it, GT, GT))
                    dve.wait_ge(tl.y_ready, before(it + tl.turn0))
                    dve.tensor_copy(oh[:], sq[:]).then_inc(oh_ready, 1)
                    dve.wait_ge(oh_ready, now(it))
                    dve.tensor_tensor(ol[:], sq[:], oh[:].bitcast(F32), ALU.subtract).then_inc(ol_ready, 1)
                    if ahead:
                        start(it + 1)
                    tail_norm_dve(dve, tl, it, add=True)
                    tail_split_dve(dve, tl, it)

                start(0)
                with dve.Fori(0, NCH - 1) as it:
                    chunk(it, ahead=True)
                chunk(NCH - 1, ahead=False)


def ffn_weights(nc, octx, t, sem):
    def sb(name, shape, dt=F32R):
        return octx.enter_context(nc.sbuf_tensor(name, shape, dt))

    gu = 2 * FT * P
    wguh, wgul = sb("wguh", [P, KD, gu]), sb("wgul", [P, KD, gu])
    wrh, wrl = sb("wrh", [P, KD, NE]), sb("wrl", [P, KD, NE])
    selcw = sb("selcw", [NE, FT, P])
    lower = sb("lower", [P, NE * NE], F32)
    f_in, f_dve = sem("f_in"), sem("f_dve")
    f_in1, f_small, f_act = sem("f_in1"), sem("f_small"), sem("f_act")
    half = gu // 2
    with nc.sbuf_tensor("gu_raw", [P, KD, gu], F32) as gu_raw, \
         nc.sbuf_tensor("r_raw", [P, KD, NE], F32) as r_raw, nc.sbuf_tensor("s_raw", [NE, FT, P], F32) as s_raw:
        with nc.Block() as block:
            @block.sync
            def _(sp):
                for k in range(KD):
                    sp.dma_start(gu_raw[:, k], t["wgu"][k * P:(k + 1) * P]).then_inc(f_in if k == 0 else f_in1, 16)
                sp.dma_start(r_raw[:], t["wr"].rearrange("(k p) m -> p k m", p=P)).then_inc(f_small, 16)
                sp.dma_start(s_raw[:], t["selcw"]).then_inc(f_small, 16)
                sp.dma_start(lower[:], t["lower"].broadcast_to([P, NE * NE])).then_inc(f_small, 16)

            @block.scalar
            def _(act):
                act.wait_ge(f_in1, 16)
                act.activation(wguh[:, 1, half:], gu_raw[:, 1, half:], ACT.Copy).then_inc(f_act, 1)
                act.activation(wguh[:, 1, :half], gu_raw[:, 1, :half], ACT.Copy).then_inc(f_act, 1)

            @block.vector
            def _(dve):
                dve.wait_ge(f_in, 16)
                dve.tensor_copy(wguh[:, 0], gu_raw[:, 0]).then_inc(f_dve, 1)
                dve.wait_ge(f_dve, 1)
                dve.tensor_tensor(wgul[:, 0], gu_raw[:, 0], wguh[:, 0].bitcast(F32), ALU.subtract)
                dve.wait_ge(f_small, 48)
                dve.tensor_copy(selcw[:], s_raw[:])
                dve.tensor_copy(wrh[:], r_raw[:]).then_inc(f_dve, 1)
                dve.wait_ge(f_dve, 2)
                dve.tensor_tensor(wrl[:], r_raw[:], wrh[:].bitcast(F32), ALU.subtract)
                dve.wait_ge(f_act, 2)
                dve.tensor_tensor(wgul[:, 1, :half], gu_raw[:, 1, :half], wguh[:, 1, :half].bitcast(F32), ALU.subtract)

            @block.gpsimd
            def _(pool):
                pool.wait_ge(f_act, 1)
                pool.tensor_tensor(wgul[:, 1, half:], gu_raw[:, 1, half:], wguh[:, 1, half:].bitcast(F32), ALU.subtract)
    return wguh, wgul, wrh, wrl, selcw, lower


def experts(nc, t, wts, x, xTh, xTl, yT, psY, bank, tl, stand, credit, tail_norm_dve, tail_split_dve,
            tail_pool, tail_pe, tail_act, osem, ident, xcols, ffn_sems, last, out=None, stored=None):
    wguh, wgul, wrh, wrl, selcw, lower = wts
    ph = "2" if last else "1"

    def sem(name):
        if name not in ffn_sems:
            ffn_sems[name] = osem(name)
        return ffn_sems[name]
    ctx = ExitStack()
    with ctx:
        def sb(name, shape, dt=F32):
            return ctx.enter_context(nc.sbuf_tensor(name + ph, shape, dt))

        wd_raw = sb("wd_raw", [P, FT, D])
        wdh, wdl = sb("wdh", [P, FT, D], F32R), sb("wdl", [P, FT, D], F32R)
        lg = sb("lg", [NE, CH])
        L = sb("L", [P, TPC, NE])
        top = sb("top", [P, TPC])
        cmp1, cmp2 = sb("cmp1", [P, TPC, NE * NE]), sb("cmp2", [P, TPC, NE * NE])
        rank = sb("rank", [P, TPC, NE])
        chosen = sb("chosen", [P, TPC, NE])
        ex = sb("ex", [P, TPC, NE])
        den, rden = sb("den", [P, TPC]), sb("rden", [P, TPC])
        cw = sb("cw", [P, TPC, NE])
        cwh, cwl = sb("cwh", [NE, CH], F32R), sb("cwl", [NE, CH], F32R)
        silu = sb("silu", [P, 2, CH])
        act_up = sb("act_up", [P, 2, CH])
        hid = sb("hid", [P, 2, CH])
        hh, hl = sb("hh", [P, 2, CH], F32R), sb("hl", [P, 2, CH], F32R)
        psG, psU, psB = bank[0], bank[1], bank[2]

        lg_ready = sem("lg_ready")
        lgT_ready = sem("lgT_ready")
        cwT_ready = sem("cwT_ready")
        g_ready = sem("g_ready")
        u_ready = sem("u_ready")
        b_ready = sem("b_ready")
        down_done = sem("down_done")
        lg_out = sem("lg_out")
        exp_done = sem("exp_done")
        silu_done = sem("silu_done")
        hh_done = sem("hh_done")
        route = sem("route")
        cwl_done = sem("cwl_done")
        up_done = sem("up_done")
        hid_done = sem("hid_done")
        hl_done = sem("hl_done")
        wd_in = sem("wd_in")
        wd_done = sem("wd_done")
        NR = 13
        turns = NCH if last else 0

        with nc.Block() as block:
            @block.tensor
            def _(pe):
                if not last:
                    credit(pe, (lg_ready, 1), (lgT_ready, 1), (cwT_ready, 1), (g_ready, FT), (u_ready, FT),
                           (b_ready, FT), (down_done, FT))
                def project(it, dst, wh, wl, c0, c1):
                    n = 0
                    for k in range(KD):
                        for wt, xx in ((wh, xTh), (wl, xTh), (wh, xTl)):
                            mm = pe.matmul(dst, wt[:, k, c0:c1], xx[:, k, bass.ds(it * CH, CH)],
                                           start=n == 0, stop=n == 3 * KD - 1)
                            n += 1
                    return mm

                def gate_up(it, i):
                    r = it + turns
                    pe.wait_ge(silu_done, now(r, i - 1, FT))
                    project(it, psG[:, i % 2], wguh, wgul, i * P, (i + 1) * P).then_inc(g_ready, 1)
                    pe.wait_ge(up_done, now(r, i - 1, FT))
                    project(it, psU[:, i % 2], wguh, wgul, (FT + i) * P, (FT + i + 1) * P).then_inc(u_ready, 1)

                def head(it, tail_of=None):
                    r = it + turns
                    pe.wait_ge(hid_done, before(r, FT, FT))
                    stand(pe)
                    project(it, psB[0:NE, 0], wrh, wrl, 0, NE).then_inc(lg_ready, 1)
                    gate_up(it, 0)
                    pe.wait_ge(lg_out, now(r))
                    stand(pe)
                    for j in range(TPC):
                        mm = pe.transpose(psB[:, 1, j * NE:(j + 1) * NE], lg[:, j * P:(j + 1) * P],
                                          ident[0:NE, 0:NE])
                    mm.then_inc(lgT_ready, 1)
                    gate_up(it, 1)
                    if tail_of is not None:
                        tail_pe(pe, tl, tail_of)
                    pe.wait_ge(route, now(r, NR, NR))
                    for j in range(TPC):
                        mm = pe.transpose(psB[0:NE, 1, j * P:(j + 1) * P], cw[:, j], ident[:])
                    mm.then_inc(cwT_ready, 1)

                def down(it, i):
                    r = it + turns
                    pe.wait_ge(hl_done, now(r, i + 1, FT))
                    if i == 0:
                        pe.wait_ge(wd_done, 2 * last + 2)
                        pe.wait_ge(tl.xl_ready, before(it + tl.turn0))
                    for j in range(TPC):
                        for n, (h, w) in enumerate(((hh, wdh), (hl, wdh), (hh, wdl))):
                            mm = pe.matmul(yT[:, j * D:(j + 1) * D], h[:, i % 2, j * P:(j + 1) * P], w[:, i],
                                           start=i == 0 and n == 0 and j % 2 == 0,
                                           stop=i == FT - 1 and n == 2, skip_group_check=True)
                    mm.then_inc(down_done, 1)

                def tiles(it):
                    r = it + turns
                    pe.wait_ge(cwl_done, now(r, 2, 2))
                    for i in range(FT):
                        pe.wait_ge(hid_done, now(r, i - 1, FT))
                        pe.matmul(psB[:, i % 2], selcw[:, i], cwh[:], start=True, stop=False)
                        pe.matmul(psB[:, i % 2], selcw[:, i], cwl[:], start=False, stop=True).then_inc(b_ready, 1)
                        if i >= 1:
                            down(it, i - 1)
                        if i + 2 < FT:
                            gate_up(it, i + 2)
                    down(it, FT - 1)
                    pe.wait_ge(down_done, now(r, FT, FT))
                    pe.sem_inc(tl.y_ready, 1)

                head(0)
                with pe.Fori(0, NCH - 1) as it:
                    tiles(it)
                    head(it + 1, tail_of=None if last else it)
                tiles(NCH - 1)
                if not last:
                    tail_pe(pe, tl, NCH - 1)

            @block.scalar
            def _(act):
                if not last:
                    credit(act, (lg_out, 1), (exp_done, 1), (silu_done, FT), (hh_done, FT))
                def gate(it, i):
                    r = it + turns
                    act.wait_ge(g_ready, now(r, i + 1, FT))
                    act.wait_ge(up_done, now(r, i - 1, FT))
                    act.activation(silu[:, i % 2], psG[:, i % 2], ACT.Silu).then_inc(silu_done, 1)

                def head(it, tail_of=None):
                    r = it + turns
                    act.wait_ge(lg_ready, now(r))
                    act.wait_ge(lgT_ready, before(r))
                    act.activation(lg[:], psB[0:NE, 0], ACT.Copy).then_inc(lg_out, 1)
                    gate(it, 0)
                    gate(it, 1)
                    if tail_of is not None:
                        tail_act(act, tl, tail_of)
                    act.wait_ge(route, now(r, 7, NR))
                    act.activation(ex[:], ex[:], ACT.Exp).then_inc(exp_done, 1)

                def tiles(it):
                    r = it + turns
                    for i in range(FT):
                        act.wait_ge(hid_done, now(r, i + 1, FT))
                        act.wait_ge(down_done, now(r, i - 1, FT))
                        act.activation(hh[:, i % 2], hid[:, i % 2], ACT.Copy).then_inc(hh_done, 1)
                        if i + 2 < FT:
                            gate(it, i + 2)

                head(0)
                with act.Fori(0, NCH - 1) as it:
                    tiles(it)
                    head(it + 1, tail_of=None if last else it)
                tiles(NCH - 1)
                if not last:
                    tail_act(act, tl, NCH - 1)

            @block.sync
            def _(sp):
                sp.dma_start(wd_raw[:], t["wd"].rearrange("(k p) m -> p k m", p=P)).then_inc(wd_in, 16)
                if last:
                    for c in range(NCH):
                        rows = slice(c * TPC, (c + 1) * TPC)
                        sp.wait_ge(tl.xl_ready, now(c + tl.turn0))
                        sp.dma_start(out.rearrange("(t p) d -> p t d", p=P)[:, rows],
                                     xcols(c).rearrange("p (t d) -> p t d", d=D)).then_inc(stored, 16)
                    sp.wait_ge(stored, 16 * NCH)

            @block.gpsimd
            def _(pool):
                pool.wait_ge(wd_in, 16 * (1 + last))
                pool.tensor_copy(wdh[:], wd_raw[:]).then_inc(wd_done, 1)
                pool.wait_ge(wd_done, 2 * last + 1)
                pool.tensor_tensor(wdl[:], wd_raw[:], wdh[:].bitcast(F32), ALU.subtract).then_inc(wd_done, 1)
                if not last:
                    with pool.Fori(0, NCH) as it:
                        tail_pool(pool, tl, it)

            @block.vector
            def _(dve):
                if not last:
                    credit(dve, (route, NR), (cwl_done, 2), (up_done, FT), (hid_done, FT), (hl_done, FT))
                def up(it, i):
                    r = it + turns
                    dve.wait_ge(u_ready, now(r, i + 1, FT))
                    dve.wait_ge(silu_done, now(r, i + 1, FT))
                    dve.wait_ge(hid_done, now(r, i - 1, FT))
                    dve.tensor_tensor(act_up[:, i % 2], silu[:, i % 2], psU[:, i % 2], ALU.mult)\
                       .then_inc(up_done, 1)

                def routing(it, split_of=None):
                    r = it + turns
                    n = 0

                    def step(ins):
                        nonlocal n
                        n += 1
                        ins.then_inc(route, 1)
                        dve.wait_ge(route, now(r, n, NR))

                    by_e = L[:].unsqueeze(3).broadcast_to([P, TPC, NE, NE])
                    by_j = L[:].unsqueeze(2).broadcast_to([P, TPC, NE, NE])
                    low = lower[:].unsqueeze(1).broadcast_to([P, TPC, NE * NE])
                    c1 = cmp1[:].rearrange("p t (e j) -> p t e j", e=NE)
                    c2 = cmp2[:].rearrange("p t (e j) -> p t e j", e=NE)
                    dve.wait_ge(lgT_ready, now(r))
                    step(dve.tensor_copy(L[:], psB[:, 1, 0:TPC * NE].rearrange("p (t e) -> p t e", e=NE)))
                    step(dve.tensor_tensor(c1, by_j, by_e, ALU.is_ge))
                    step(dve.tensor_tensor(cmp1[:], cmp1[:], low, ALU.mult))
                    step(dve.tensor_tensor(c2, by_j, by_e, ALU.is_gt))
                    step(dve.tensor_tensor(cmp1[:], cmp1[:], cmp2[:], ALU.max))
                    step(dve.tensor_reduce(top[:], L[:], AX.X, ALU.max))
                    step(dve.tensor_tensor(ex[:], L[:], top[:].unsqueeze(2).broadcast_to([P, TPC, NE]), ALU.subtract))
                    step(dve.tensor_reduce(rank[:], c1, AX.X, ALU.add))
                    step(dve.tensor_scalar(chosen[:], rank[:], 1.5, None, ALU.is_lt))
                    dve.wait_ge(exp_done, now(r))
                    step(dve.tensor_tensor(chosen[:], chosen[:], ex[:], ALU.mult))
                    step(dve.tensor_reduce(den[:], chosen[:], AX.X, ALU.add))
                    step(dve.reciprocal(rden[:], den[:]))
                    step(dve.tensor_tensor(cw[:], chosen[:], rden[:].unsqueeze(2).broadcast_to([P, TPC, NE]), ALU.mult))
                    assert n == NR
                    if split_of is not None:
                        tail_split_dve(dve, tl, split_of)
                    up(it, 0)
                    up(it, 1)
                    dve.wait_ge(cwT_ready, now(r))
                    dve.tensor_copy(cwh[:], psB[0:NE, 1]).then_inc(cwl_done, 1)
                    dve.wait_ge(cwl_done, now(r, 1, 2))
                    dve.tensor_tensor(cwl[:], psB[0:NE, 1], cwh[:].bitcast(F32), ALU.subtract).then_inc(cwl_done, 1)

                def tiles(it):
                    r = it + turns
                    for i in range(FT):
                        dve.wait_ge(b_ready, now(r, i + 1, FT))
                        dve.wait_ge(up_done, now(r, i + 1, FT))
                        dve.tensor_tensor(hid[:, i % 2], act_up[:, i % 2], psB[:, i % 2], ALU.mult)\
                           .then_inc(hid_done, 1)
                        dve.wait_ge(hh_done, now(r, i + 1, FT))
                        dve.tensor_tensor(hl[:, i % 2], hid[:, i % 2], hh[:, i % 2].bitcast(F32), ALU.subtract)\
                           .then_inc(hl_done, 1)
                        if i + 2 < FT:
                            up(it, i + 2)

                def tail(it, split):
                    if last:
                        dve.wait_ge(tl.y_ready, now(it + tl.turn0))
                        dve.tensor_tensor(xcols(it), yT, xcols(it), ALU.add).then_inc(tl.xl_ready, 1)
                    else:
                        tail_norm_dve(dve, tl, it, add=True)
                        if split:
                            tail_split_dve(dve, tl, it)

                routing(0)
                with dve.Fori(0, NCH - 1) as it:
                    tiles(it)
                    tail(it, split=False)
                    routing(it + 1, split_of=None if last else it)
                tiles(NCH - 1)
                tail(NCH - 1, split=True)


def host_inputs(a):
    ev = np.arange(HV // 2) * 2
    E0 = np.concatenate([h * HV + ev for h in range(4)])
    E1 = np.concatenate([h * HV + ev for h in (4, 5)])
    cols_f = np.concatenate([E0, E1, E1])
    cols_v = np.concatenate([E0, E0 + 1, E1, E1 + 1, E1 + 1, E1])
    cols_g = cols_v[:GT * P]
    inv_freq = (np.float32(1.0) / np.float32(10000.0) ** (np.arange(0, HV, 2, dtype=np.float32) / np.float32(HV)))
    freq = (inv_freq[(cols_f % HV) // 2].astype(np.float64) / (2 * np.pi)).astype(np.float32)[None, :]
    g = lambda n: np.asarray(a["L0_attn_a_" + n])
    sel = np.zeros((2 * HA, 4, P), np.float32)
    selr = np.zeros((8, 2, P), np.float32)
    headsum = np.zeros((P, 2, 8), np.float32)
    for u in range(UNITS):
        for p, h in enumerate(heads_of_tile(u)):
            sel[h, u, p] = 1.0
            sel[HA + h, 2 + u, p] = 1.0
            selr[h, u, p] = 1.0
            headsum[p, u, h] = 1.0 / HV
    sscale = np.empty((P, 2), np.float32)
    sscale[:64, 0], sscale[64:, 0] = -TWO_PI, TWO_PI
    sscale[:, 1] = np.pi / 2
    return {
        "x": g("hidden_states").reshape(T, D),
        "ident": np.eye(P, dtype=np.float32),
        "wq": g("Wq")[:, cols_f], "wk": g("Wk")[:, cols_f],
        "cq": g("conv_q")[cols_f].T, "ck": g("conv_k")[cols_f].T, "freq": freq,
        "wv": g("Wv")[:, cols_v], "wg": g("Wg")[:, cols_g], "wo": g("Wo")[cols_g],
        "wab": np.concatenate([g("Wa"), g("Wb")], 1),
        "sel": sel, "selr": selr, "headsum": headsum,
        "convv": g("conv_v")[cols_v].reshape(VT, P, TAPS).transpose(1, 0, 2),
        "rmsw": g("rms_w")[cols_g % HV].reshape(GT, P).T,
        "sscale": sscale,
        **expert_inputs(a), **attention_inputs(a),
    }


def expert_inputs(a):
    gup = np.asarray(a["L0_ffn_gate_up_proj"])
    selcw = np.zeros((NE, FT, P), np.float32)
    for c in range(FT * P):
        selcw[c // FH, c // P, c % P] = 1.0
    lower = (np.arange(NE)[None, :] < np.arange(NE)[:, None]).astype(np.float32).reshape(1, -1)
    return {
        "wgu": np.concatenate([gup[:, :FH].reshape(NE * FH, D), gup[:, FH:].reshape(NE * FH, D)], 0).T,
        "wd": np.asarray(a["L0_ffn_down_proj"]).transpose(0, 2, 1).reshape(NE * FH, D),
        "wr": np.asarray(a["L0_ffn_router_w"]).T,
        "selcw": selcw, "lower": lower,
    }


def attention(nc, t, x, xTh, xTl, yT, psY, bank, tl, stand, credit, tail_norm_dve, tail_split_dve,
              tail_pool, tail_pe, tail_act, sem, ident):
    ctx = ExitStack()
    NPAIR = TPC * HB // 2
    PPB = HB // 2
    SLOTS = HB // 2
    ROWS = 64 + STK
    SCALE = HD ** -0.5
    BS = P + PERSIST
    KC = (TPC + 1) * BS
    with ctx:
        def sb(name, shape, dt=F32):
            return ctx.enter_context(nc.sbuf_tensor("b_" + name, shape, dt))

        shapes = {"bq": [P, KD, D], "bkv": [P, KD, LAT], "bk": [LAT, D], "bv": [LAT, D], "bo": [P, KD, D]}
        wh = {n: sb(n + "h", shapes[n], F32R) for n in shapes}
        wl = {n: sb(n + "l", shapes[n], F32R) for n in shapes}
        masks = sb("masks", [P, TPC, WIN])
        lath, latl = sb("lath", [LAT, CH], F32R), sb("latl", [LAT, CH], F32R)
        qh, ql = sb("qh", [P, KD, CH], F32R), sb("ql", [P, KD, CH], F32R)
        kh, kl = sb("kh", [P, KD, TPC * BS], F32R), sb("kl", [P, KD, TPC * BS], F32R)

        def own_keys(w):
            return w[:].rearrange("p k (b c) -> p (k b) c", c=BS)[:, :, 0:P]

        QS = sb("QS", [ROWS, SLOTS, CH], F32R)
        KS = sb("KS", [ROWS, SLOTS, KC], F32R)
        V = sb("V", [P, TPC + 1, D])
        vp = sb("vp", [PERSIST, D])
        VP = sb("VP", [P, 2, P])
        sm = sb("sm", [P, 4, WIN])
        mx, nmx = sb("mx", [P, 4]), sb("nmx", [P, 4])
        prob = sb("prob", [P, 8, WIN])
        pp = sb("pp", [P, 2, HB, PERSIST])
        rs = sb("rs", [P, 2, HB])
        rinv = sb("rinv", [P, HB])
        pT = sb("pT", [P, 2, 4 * P])
        ppT = sb("ppT", [P, 2 * P])
        on = sb("on", [P, D])
        oTh, oTl = qh, ql
        raw = {"bq": pT[:, 0].rearrange("p (k c) -> p k c", k=KD), "bo": pT[:, 1].rearrange("p (k c) -> p k c", k=KD),
               "bk": on[0:LAT], "bv": ppT[0:LAT],
               "bkv": pp[:, 0, 0:2 * LAT // PERSIST].rearrange("p (k a) b -> p k (a b)", k=KD)}
        zeros = sm[:].rearrange("p a b -> p (a b)")[:, 0:KC]

        psS = [bank[0][:, 0], bank[0][:, 1], bank[1][:, 0], bank[1][:, 1]]
        psT = bank[2]
        psO, psM = psY[:, 0], psY[:, 1]

        b_in = sem("b_in")
        b_prep = sem("b_prep")
        p_lat, p_latl, p_k, p_kl, p_v = (sem("p_" + n) for n in ("lat", "latl", "k", "kl", "v"))
        p_stk = sem("p_stk")
        with nc.Block() as block:
            stack = ((0, 0), (1, 0), (2, 1))

            @block.sync
            def _(sp):
                for n in raw:
                    sp.dma_start(raw[n], t[n].rearrange("(k p) m -> p k m", p=P) if n in ("bq", "bkv", "bo") else t[n])\
                      .then_inc(b_in, 16)
                sp.dma_start(masks[:], t["masks"]).then_inc(b_in, 16)
                sp.wait_ge(p_kl, 2)
                for half in range(2):
                    for blk, part in stack:
                        src = (kh, kl)[part][64 * half:64 * half + 64, :, P:BS]
                        sp.dma_start(KS[64 * half + HD * blk:64 * half + HD * blk + HD, :, P:BS].bitcast(F32),
                                     src.bitcast(F32)).then_inc(p_stk, 16)
                sp.wait_ge(p_v, 2)
                for r in range(HG):
                    sp.dma_start(VP[HD * r:HD * r + PERSIST, :, HD * r:HD * r + HD],
                                 vp[:].rearrange("p (g c) -> p g c", g=2)[:, :, r * HD:(r + 1) * HD])\
                      .then_inc(p_stk, 16)
                sp.wait_ge(p_stk, 16 * (6 + HG))

            @block.vector
            def _(dve):
                n = 0

                def link(ins):
                    nonlocal n
                    n += 1
                    ins.then_inc(b_prep, 1)
                    dve.wait_ge(b_prep, n)
                link(dve.memset(VP[:], 0.0))
                link(dve.memset(V[:, TPC], 0.0))
                link(dve.memset(zeros, 0.0))
                for s in range(SLOTS):
                    link(dve.tensor_copy(KS[:, s], zeros[0:ROWS]))
                dve.wait_ge(b_in, 16 * (len(raw) + 1))
                for m in raw:
                    link(dve.tensor_copy(wh[m][:], raw[m]))
                    link(dve.tensor_tensor(wl[m][:], raw[m], wh[m][:].bitcast(F32), ALU.subtract))
                dve.wait_ge(p_lat, 1)
                dve.tensor_copy(lath[:, 0:PERSIST], psM[0:LAT, 0:PERSIST]).then_inc(p_latl, 1)
                dve.wait_ge(p_latl, 1)
                dve.tensor_tensor(latl[:, 0:PERSIST], psM[0:LAT, 0:PERSIST], lath[:, 0:PERSIST].bitcast(F32),
                                  ALU.subtract).then_inc(p_latl, 1)
                dve.wait_ge(p_k, 1)
                dve.tensor_copy(kh[:, :, P:BS], bank[0][:, :, 0:PERSIST]).then_inc(p_kl, 1)
                dve.wait_ge(p_kl, 1)
                dve.tensor_tensor(kl[:, :, P:BS], bank[0][:, :, 0:PERSIST], kh[:, :, P:BS].bitcast(F32),
                                  ALU.subtract).then_inc(p_kl, 1)
                dve.tensor_copy(vp[:], bank[1][0:PERSIST, 0, 0:D]).then_inc(p_v, 2)
                dve.wait_ge(p_kl, 2)
                for w in (kh, kl):
                    for b in range(1, TPC):
                        dve.tensor_copy(w[:, :, b * BS + P:(b + 1) * BS], w[:, :, P:BS])

            @block.tensor
            def _(pe):
                pe.wait_ge(b_prep, 2 + 1 + SLOTS + 2 * len(raw))
                n = 0
                for k in range(KD):
                    for w, xx in ((wh, xTh), (wl, xTh), (wh, xTl)):
                        mm = pe.matmul(psM[0:LAT, 0:PERSIST], w["bkv"][:, k], xx[:, k, 0:PERSIST],
                                       start=n == 0, stop=n == 3 * KD - 1)
                        n += 1
                mm.then_inc(p_lat, 1)
                pe.wait_ge(p_latl, 2)
                for n, (w, z) in enumerate(((wh, lath), (wl, lath), (wh, latl))):
                    mm = pe.matmul(bank[1][0:PERSIST, 0, 0:D], z[:, 0:PERSIST], w["bv"][:], start=n == 0, stop=n == 2)
                for g in range(KD):
                    for n, (w, z) in enumerate(((wh, lath), (wl, lath), (wh, latl))):
                        mm = pe.matmul(bank[0][:, g, 0:PERSIST], w["bk"][:, g * P:(g + 1) * P], z[:, 0:PERSIST],
                                       start=n == 0, stop=n == 2)
                mm.then_inc(p_k, 1)

        lat_ready = sem("lat_ready")
        q_ready = sem("q_ready")
        k_ready = sem("k_ready")
        v_ready = sem("v_ready")
        s_ready = sem("s_ready")
        t_ready = sem("t_ready")
        pv_done = sem("pv_done")
        pt_ready = sem("pt_ready")
        o_ready = sem("o_ready")
        oT_ready = sem("oT_ready")
        lath_done = sem("lath_done")
        qh_done, kh_done = sem("qh_done"), sem("kh_done")
        v_done = sem("v_done")
        e_done = sem("e_done")
        ta_out = sem("ta_out")
        oh_done = sem("boh_done")
        latl_done = sem("latl_done")
        ql_done, kl_done = sem("ql_done"), sem("kl_done")
        m_done = sem("m_done")
        n_done = sem("n_done")
        tv_out = sem("tv_out")
        pp_out = sem("pp_out")
        ri_done = sem("ri_done")
        on_done = sem("on_done")
        ol_done = sem("bol_done")
        mask_done = sem("mask_done")
        halo_done = sem("bhalo_done")
        vhalo_done = sem("vhalo_done")
        pp_done = sem("pp_done")
        stacked = sem("stacked")
        NS = 16 * 12

        STEPS = NPAIR + 6

        def ends_block(p):
            return 0 <= p < NPAIR and p % PPB == PPB - 1

        with nc.Block() as block:
            @block.tensor
            def _(pe):
                credit(pe, (lat_ready, 1), (q_ready, 1), (k_ready, 1), (v_ready, 1), (s_ready, NPAIR),
                       (t_ready, NPAIR), (pv_done, NPAIR), (pt_ready, TPC), (o_ready, TPC), (oT_ready, TPC))
                def project(it, dst, m, c0, c1):
                    n = 0
                    for k in range(KD):
                        for w, xx in ((wh, xTh), (wl, xTh), (wh, xTl)):
                            mm = pe.matmul(dst, w[m][:, k, c0:c1], xx[:, k, bass.ds(it * CH, CH)],
                                           start=n == 0, stop=n == 3 * KD - 1)
                            n += 1
                    return mm

                def latent_and_queries(it):
                    project(it, psT[0:LAT, 0], "bkv", 0, LAT).then_inc(lat_ready, 1)
                    for g in range(KD):
                        mm = project(it, bank[0][:, g], "bq", g * P, (g + 1) * P)
                    mm.then_inc(q_ready, 1)

                def chunk(it, ahead):
                    pe.wait_ge(latl_done, now(it))
                    for g in range(KD):
                        for n, (w, z) in enumerate(((wh, lath), (wl, lath), (wh, latl))):
                            mm = pe.matmul(bank[1][:, g], w["bk"][:, g * P:(g + 1) * P], z[:], start=n == 0, stop=n == 2)
                    mm.then_inc(k_ready, 1)
                    for j in range(TPC):
                        for n, (w, z) in enumerate(((wh, lath), (wl, lath), (wh, latl))):
                            mm = pe.matmul(psT[:, j // 2, (j % 2) * D:(j % 2 + 1) * D], z[:, j * P:(j + 1) * P],
                                           w["bv"][:], start=n == 0, stop=n == 2)
                    mm.then_inc(v_ready, 1)
                    pe.wait_ge(tl.xl_ready, before(it + tl.turn0))
                    pe.wait_ge(stacked, (it + 1) * NS)
                    pe.wait_ge(kl_done, now(it))
                    pe.wait_ge(ql_done, now(it))
                    pe.wait_ge(v_done, now(it))
                    for s in range(STEPS):
                        if s < NPAIR:
                            b = s // PPB
                            pe.wait_ge(m_done, now(it, s - 1, NPAIR))
                            for i in range(2):
                                h = 2 * (s % PPB) + i
                                g, half, j = h // HG, (h % HG) // 4, h % 4
                                rows = slice(64 * half, 64 * half + STK)
                                dst = psS[2 * (s % 2) + i]
                                q = QS[rows, KD * j + g, b * P:(b + 1) * P]
                                mm = pe.matmul(dst[:, 0:WIN], q, KS[rows, KD * j + g, b * BS:b * BS + WIN],
                                               start=True, stop=True)
                            mm.then_inc(s_ready, 1)
                        p = s - 2
                        if 0 <= p < NPAIR:
                            b = p // PPB
                            pe.wait_ge(e_done, now(it, 2 * p + 2, 2 * NPAIR))
                            if p % 2 == 0:
                                pe.wait_ge(tv_out, now(it, p // 2, NPAIR // 2))
                            else:
                                pe.wait_ge(ta_out, now(it, p // 2, NPAIR // 2))
                            for i in range(2):
                                for c in range(2):
                                    mm = pe.transpose(psT[:, p % 2, (2 * i + c) * P:(2 * i + c + 1) * P],
                                                      prob[:, 2 * (p % 4) + i,
                                                           c * BS:c * BS + P], ident[:])
                            mm.then_inc(t_ready, 1)
                            if ends_block(p):
                                pe.wait_ge(pp_done, now(it, p + 1, NPAIR))
                                pe.wait_ge(ol_done, now(it, b, TPC))
                                if b == 0:
                                    pe.wait_ge(tl.xl_ready, before(it + tl.turn0))
                                for g in range(2):
                                    mm = pe.transpose(psM[:, g * P:(g + 1) * P],
                                                      pp[:, b % 2, g * HG:(g + 1) * HG], ident[:])
                                mm.then_inc(pt_ready, 1)
                        p = s - 3
                        if 0 <= p < NPAIR:
                            b = p // PPB
                            if p % 2 == 0:
                                pe.wait_ge(tv_out, now(it, p // 2 + 1, NPAIR // 2))
                            else:
                                pe.wait_ge(ta_out, now(it, p // 2 + 1, NPAIR // 2))
                            if p % PPB == 0:
                                pe.wait_ge(on_done, now(it, b, TPC))
                            for i in range(2):
                                h = 2 * (p % PPB) + i
                                for c in range(2):
                                    mm = pe.matmul(psO[:, (b % 2) * D + h * HD:(b % 2) * D + (h + 1) * HD],
                                                   pT[:, p % 2, (2 * i + c) * P:(2 * i + c + 1) * P],
                                                   V[:, b + c, h * HD:(h + 1) * HD],
                                                   start=h == 0 and c == 0, stop=False, skip_group_check=True)
                            mm.then_inc(pv_done, 1)
                            if ends_block(p):
                                pe.wait_ge(pp_out, now(it, b + 1, TPC))
                                for g in range(2):
                                    mm = pe.matmul(psO[:, (b % 2) * D + g * P:(b % 2) * D + (g + 1) * P],
                                                   ppT[:, g * P:(g + 1) * P], VP[:, g], start=False, stop=True,
                                                   skip_group_check=True)
                                mm.then_inc(o_ready, 1)
                        p = s - 5
                        if ends_block(p):
                            b = p // PPB
                            pe.wait_ge(on_done, now(it, b + 1, TPC))
                            for k in range(KD):
                                mm = pe.transpose(psM[:, (2 + k) * P:(3 + k) * P], on[:, k * P:(k + 1) * P], ident[:])
                            mm.then_inc(oT_ready, 1)
                    pe.wait_ge(ol_done, now(it, TPC, TPC))
                    for i in range(TPC):
                        n = 0
                        for k in range(KD):
                            for oo, w in ((oTh, wh), (oTl, wh), (oTh, wl)):
                                mm = pe.matmul(yT[:, i * D:(i + 1) * D], oo[:, k, i * P:(i + 1) * P], w["bo"][:, k],
                                               start=n == 0, stop=n == 3 * KD - 1)
                                n += 1
                    mm.then_inc(tl.y_ready, 1)
                    if ahead:
                        latent_and_queries(it + 1)
                    tail_pe(pe, tl, it)

                latent_and_queries(0)
                with pe.Fori(0, NCH - 1) as it:
                    chunk(it, ahead=True)
                chunk(NCH - 1, ahead=False)

            @block.sync
            def _(sp):
                with sp.Fori(0, NCH) as it:
                    sp.wait_ge(s_ready, before(it, NPAIR, NPAIR))
                    stand(sp)
                    sp.wait_ge(halo_done, now(it))
                    stand(sp)
                    for to_k, first, done, parts in ((False, (qh, ql), ql_done, (0, 1, 0)),
                                                     (True, (kh, kl), kl_done, (0, 0, 1))):
                        sp.wait_ge(done, now(it))
                        stand(sp)
                        for half in range(2):
                            for blk in range(3):
                                rows = slice(64 * half + HD * blk, 64 * half + HD * blk + HD)
                                src = first[parts[blk]][64 * half:64 * half + 64]
                                dst = KS[rows, :, BS:] if to_k else QS[rows]
                                sp.dma_start(dst.bitcast(F32), src.bitcast(F32)).then_inc(stacked, 16)

            @block.gpsimd
            def _(pool):
                credit(pool, (halo_done, 1), (vhalo_done, 1), (pp_done, NPAIR))
                with pool.Fori(0, NCH) as it:
                    pool.wait_ge(s_ready, before(it, NPAIR, NPAIR))
                    stand(pool)
                    pool.tensor_copy(KS[:, :, 0:P], KS[:, :, TPC * BS:TPC * BS + P]).then_inc(halo_done, 1)
                    pool.wait_ge(pv_done, before(it, NPAIR, NPAIR))
                    stand(pool)
                    pool.tensor_copy(V[:, 0], V[:, TPC]).then_inc(vhalo_done, 1)
                    for s in range(NPAIR):
                        b = s // PPB
                        pool.wait_ge(e_done, now(it, 2 * s + 2, 2 * NPAIR))
                        if s % PPB == 0:
                            pool.wait_ge(pt_ready, now(it, b - 1, TPC))
                        h = 2 * (s % PPB)
                        stand(pool)
                        pool.tensor_copy(pp[:, b % 2, h:h + 2], prob[:, 2 * (s % 4):2 * (s % 4) + 2, P:BS])\
                            .then_inc(pp_done, 1)
                    tail_pool(pool, tl, it)

            @block.scalar
            def _(act):
                credit(act, (lath_done, 1), (qh_done, 1), (kh_done, 1), (v_done, 1), (e_done, 2 * NPAIR),
                       (ta_out, NPAIR // 2), (oh_done, TPC))
                def latent_and_queries(it):
                    act.wait_ge(lat_ready, now(it))
                    act.activation(lath[:], psT[0:LAT, 0], ACT.Copy).then_inc(lath_done, 1)
                    act.wait_ge(q_ready, now(it))
                    act.wait_ge(tl.y_ready, before(it + tl.turn0))
                    act.activation(qh[:], bank[0][:], ACT.Copy).then_inc(qh_done, 1)

                def chunk(it, ahead):
                    act.wait_ge(k_ready, now(it))
                    act.activation(own_keys(kh), bank[1][:].rearrange("p k (b c) -> p (k b) c", c=P), ACT.Copy).then_inc(kh_done, 1)
                    act.wait_ge(v_ready, now(it))
                    act.wait_ge(vhalo_done, now(it))
                    act.activation(V[:, 1:TPC + 1].rearrange("p a b -> p (a b)"),
                                   psT[:].rearrange("p a b -> p (a b)"), ACT.Copy).then_inc(v_done, 1)
                    for s in range(STEPS):
                        if s < NPAIR:
                            b = s // PPB
                            act.wait_ge(n_done, now(it, s + 1, NPAIR))
                            act.wait_ge(t_ready, now(it, s - 3, NPAIR))
                            act.wait_ge(pp_done, now(it, s - 3, NPAIR))
                            if s % PPB == 0:
                                act.wait_ge(ri_done, now(it, b - 1, TPC))
                            for i in range(2):
                                h = 2 * (s % PPB) + i
                                m = (2 * s + i) % 4
                                act.activation(prob[:, 2 * (s % 4) + i], sm[:, m], ACT.Exp, bias=nmx[:, m:m + 1], scale=SCALE,
                                               accum_out=rs[:, b % 2, h:h + 1]).then_inc(e_done, 1)
                        p = s - 2
                        if 0 <= p < NPAIR and p % 2 == 1:
                            act.wait_ge(t_ready, now(it, p + 1, NPAIR))
                            act.wait_ge(pv_done, now(it, p - 1, NPAIR))
                            act.activation(pT[:, 1], psT[:, 1], ACT.Copy).then_inc(ta_out, 1)
                        p = s - 5
                        if ends_block(p):
                            b = p // PPB
                            act.wait_ge(oT_ready, now(it, b + 1, TPC))
                            if b == 0:
                                act.wait_ge(tl.y_ready, before(it + tl.turn0))
                            act.activation(oTh[:, :, b * P:(b + 1) * P],
                                           psM[:, 2 * P:4 * P].rearrange("p (k c) -> p k c", k=KD), ACT.Copy)\
                               .then_inc(oh_done, 1)
                    if ahead:
                        latent_and_queries(it + 1)
                    tail_act(act, tl, it)

                latent_and_queries(0)
                with act.Fori(0, NCH - 1) as it:
                    chunk(it, ahead=True)
                chunk(NCH - 1, ahead=False)

            @block.vector
            def _(dve):
                credit(dve, (latl_done, 1), (ql_done, 1), (kl_done, 1), (m_done, NPAIR), (n_done, NPAIR),
                       (tv_out, NPAIR // 2), (pp_out, TPC), (ri_done, TPC), (on_done, TPC), (ol_done, TPC),
                       (mask_done, 1))
                def latent_and_queries(it):
                    dve.wait_ge(lath_done, now(it))
                    dve.tensor_tensor(latl[:], psT[0:LAT, 0], lath[:].bitcast(F32), ALU.subtract).then_inc(latl_done, 1)
                    dve.wait_ge(qh_done, now(it))
                    dve.tensor_tensor(ql[:], bank[0][:], qh[:].bitcast(F32), ALU.subtract).then_inc(ql_done, 1)

                def chunk(it, ahead):
                    dve.wait_ge(kh_done, now(it))
                    dve.tensor_tensor(own_keys(kl), bank[1][:].rearrange("p k (b c) -> p (k b) c", c=P), own_keys(kh).bitcast(F32),
                                      ALU.subtract).then_inc(kl_done, 1)
                    dve.wait_ge(mask_done, before(it))
                    for s in range(STEPS):
                        if s < NPAIR:
                            b = s // PPB
                            dve.wait_ge(s_ready, now(it, s + 1, NPAIR))
                            dve.wait_ge(e_done, now(it, 2 * s - 2, 2 * NPAIR))
                            stand(dve)
                            for i in range(2):
                                m = (2 * s + i) % 4
                                ins = dve.tensor_tensor_reduce(sm[:, m], psS[m][:, 0:WIN], masks[:, b], 1.0, -3.0e38,
                                                               ALU.add, ALU.max, mx[:, m:m + 1])
                            ins.then_inc(m_done, 1)
                            dve.wait_ge(m_done, now(it, s + 1, NPAIR))
                            m = (2 * s) % 4
                            dve.tensor_scalar(nmx[:, m:m + 2], mx[:, m:m + 2], -SCALE, None, ALU.mult).then_inc(n_done, 1)
                        p = s - 2
                        if 0 <= p < NPAIR and p % 2 == 0:
                            dve.wait_ge(t_ready, now(it, p + 1, NPAIR))
                            dve.wait_ge(pv_done, now(it, p - 1, NPAIR))
                            dve.tensor_copy(pT[:, 0], psT[:, 0]).then_inc(tv_out, 1)
                        if ends_block(p):
                            b = p // PPB
                            dve.wait_ge(pt_ready, now(it, b + 1, TPC))
                            dve.wait_ge(o_ready, now(it, b, TPC))
                            dve.tensor_copy(ppT[:], psM[:, 0:2 * P]).then_inc(pp_out, 1)
                            dve.reciprocal(rinv[:], rs[:, b % 2]).then_inc(ri_done, 1)
                        p = s - 3
                        if ends_block(p):
                            b = p // PPB
                            dve.wait_ge(o_ready, now(it, b + 1, TPC))
                            dve.wait_ge(ri_done, now(it, b + 1, TPC))
                            dve.wait_ge(oT_ready, now(it, b, TPC))
                            dve.tensor_tensor(on[:].rearrange("p (h d) -> p h d", d=HD),
                                              psO[:, (b % 2) * D:(b % 2 + 1) * D].rearrange("p (h d) -> p h d", d=HD),
                                              rinv[:].unsqueeze(2).broadcast_to([P, HB, HD]), ALU.mult).then_inc(on_done, 1)
                        p = s - 5
                        if ends_block(p):
                            b = p // PPB
                            dve.wait_ge(oh_done, now(it, b + 1, TPC))
                            dve.tensor_tensor(oTl[:, :, b * P:(b + 1) * P],
                                              psM[:, 2 * P:4 * P].rearrange("p (k c) -> p k c", k=KD),
                                              oTh[:, :, b * P:(b + 1) * P].bitcast(F32), ALU.subtract).then_inc(ol_done, 1)
                    dve.tensor_copy(masks[:, 0:2], masks[:, 2:4]).then_inc(mask_done, 1)
                    tail_norm_dve(dve, tl, it, add=True)
                    if ahead:
                        latent_and_queries(it + 1)
                    tail_split_dve(dve, tl, it)

                latent_and_queries(0)
                with dve.Fori(0, NCH - 1) as it:
                    chunk(it, ahead=True)
                chunk(NCH - 1, ahead=False)


def attention_inputs(a):
    g = lambda n: np.asarray(a["L0_attn_b_" + n])
    r, c = np.arange(P)[:, None], np.arange(P)[None, :]
    ok = np.zeros((P, 4, WIN), bool)
    for i in range(4):
        ok[:, i, P + PERSIST:] = c <= r
        if i > 0:
            ok[:, i, 0:P] = c > r
            ok[:, i, P:P + PERSIST] = (c <= r)[:, 0:PERSIST] if i == 1 else True
    order = np.arange(D).reshape(D // 64, 4, HD).transpose(0, 2, 1).reshape(-1)
    return {"bq": g("Wq")[:, order], "bkv": g("Wkv"), "bk": g("Wk")[:, order], "bv": g("Wv"), "bo": g("Wo"),
            "masks": np.where(ok, 0.0, MASKED).astype(np.float32)}


def kernel(**inputs):
    import concourse.bacc as bacc
    from concourse.bass_utils import run_bass_kernel_spmd

    nc = bacc.Bacc("TRN2", target_bir_lowering=False, num_devices=1)
    arrays = {f"in_{n}": np.ascontiguousarray(v) for n, v in host_inputs(inputs).items()}
    t = {n[3:]: nc.dram_tensor(n, v.shape, mybir.dt.from_np(v.dtype), kind="ExternalInput").ap()
         for n, v in arrays.items()}
    out = nc.dram_tensor("out_dram", (T, D), F32, kind="ExternalOutput").ap()
    build(nc, t, out)
    r = run_bass_kernel_spmd(nc, [arrays], core_ids=[0])
    return r.results[0]["out_dram"].reshape(1, T, D)
```
